# Optimizing a Trainium2 kernel written in Bass

```python
import numpy as np
import jax
import jax.numpy as jnp

def _softmax(x, axis=-1):
    return jax.nn.softmax(x, axis=axis)

def _gelu(x):
    return jax.nn.gelu(x, approximate=True)

def _silu(x):
    return jax.nn.silu(x)

def _sigmoid(x):
    return jax.nn.sigmoid(x)

def _layernorm(x, axis=-1, eps=1e-05):
    m = jnp.mean(x, axis=axis, keepdims=True)
    v = jnp.var(x, axis=axis, keepdims=True)
    return (x - m) / jnp.sqrt(v + eps)

def _scatter_add(tgt, idx, src, axis=0):
    return tgt.at[idx].add(src)

def _segment_sum(src, seg, n):
    return jax.ops.segment_sum(src, seg, n)
kernel_name = 'mk_gnn_resnorm_d2_gnn_r8_599f3b'

def setup_inputs(seed: int=0):
    np.random.seed(seed)
    _w = jnp.asarray

    def _rec_inputs():
        import jax
        import jax.numpy as jnp
        _gk = jax.random.key(seed)
        x = -0.0005121 + 1.001 * jax.random.normal(jax.random.fold_in(_gk, 1), (12500, 64), jnp.float32)
        src = jax.random.randint(jax.random.fold_in(_gk, 2), (200000,), 0, 12500, jnp.int32)
        dst = jax.random.randint(jax.random.fold_in(_gk, 3), (200000,), 0, 12500, jnp.int32)
        _o = jnp.argsort(dst, stable=True)
        src = src[_o]
        dst = dst[_o]
        return (x, src, dst)
    x, src, dst = _rec_inputs()

    def _L0_gnn_setup():
        import jax, jax.numpy as jnp
        import numpy as np
        N, E, D, H = (6250, 100000, 64, 4)
        NEG_SLOPE = 0.2
        EPS = 1e-16

        def _gat(x, src, dst, W, att_src, att_dst, bias, n):
            xw = (x @ W).reshape(n, H, D)
            a_src = jnp.einsum('nhc,hc->nh', xw, att_src)
            a_dst = jnp.einsum('nhc,hc->nh', xw, att_dst)
            logits = jax.nn.leaky_relu(a_src[src] + a_dst[dst], NEG_SLOPE)
            m = jax.ops.segment_max(logits, dst, num_segments=n)
            ex = jnp.exp(logits - m[dst])
            s = jax.ops.segment_sum(ex, dst, num_segments=n)
            alpha = ex / (s[dst] + EPS)
            msg = xw[src] * alpha[..., None]
            out = jax.ops.segment_sum(msg, dst, num_segments=n)
            return out.mean(axis=1) + bias
        key = jax.random.key(seed)
        ks = jax.random.split(key, 16)
        sc = 1.0 / np.sqrt(D)
        inp = {'x': jax.random.normal(ks[0], (N, D), jnp.float32), 'edge_index': jax.random.randint(ks[1], (2, E), 0, N, jnp.int64)}
        for i, tag in ((2, '1'), (9, '2')):
            inp['W' + tag] = jax.random.normal(ks[i], (D, H * D), jnp.float32) * sc
            inp['att_src' + tag] = jax.random.normal(ks[i + 1], (H, D), jnp.float32) * sc
            inp['att_dst' + tag] = jax.random.normal(ks[i + 2], (H, D), jnp.float32) * sc
            inp['b' + tag] = jnp.zeros((D,), jnp.float32)
            inp['lW' + tag] = jax.random.normal(ks[i + 3], (D, D), jnp.float32) * sc
            inp['lb' + tag] = jnp.zeros((D,), jnp.float32)
        return inp
    _L0_gnn_all = _L0_gnn_setup()
    _L0_gnn_in = {k: v for k, v in _L0_gnn_all.items() if k in ('W1', 'att_src1', 'att_dst1', 'b1', 'lW1', 'lb1', 'W2', 'att_src2', 'att_dst2', 'b2', 'lW2', 'lb2')}
    del _L0_gnn_all

    def _L1_gnn_setup():
        import jax, jax.numpy as jnp
        import numpy as np
        N_NODES = 6250
        N_EDGES = 100000
        IN_C = 64
        key = jax.random.key(seed)
        ks = jax.random.split(key, 7)
        c2 = 2 * IN_C
        return {'features': jax.random.normal(ks[0], (N_NODES, IN_C), dtype=jnp.float32), 'W_lin': jax.random.normal(ks[1], (c2, c2), dtype=jnp.float32) / np.sqrt(c2), 'b_lin': jax.random.normal(ks[2], (c2,), dtype=jnp.float32) * 0.01, 'W_out': jax.random.normal(ks[3], (IN_C, c2), dtype=jnp.float32) / np.sqrt(c2), 'b_out': jax.random.normal(ks[4], (IN_C,), dtype=jnp.float32) * 0.01, 'src': jax.random.randint(ks[5], (N_EDGES,), 0, N_NODES, dtype=jnp.int32), 'dst': jax.random.randint(ks[6], (N_EDGES,), 0, N_NODES, dtype=jnp.int32)}
    _L1_gnn_all = _L1_gnn_setup()
    _L1_gnn_in = {k: v for k, v in _L1_gnn_all.items() if k in ('W_lin', 'b_lin', 'W_out', 'b_out')}
    del _L1_gnn_all
    return {'x': x, 'src': src, 'dst': dst, 'L0_gnn_W1': _L0_gnn_in['W1'], 'L0_gnn_att_src1': _L0_gnn_in['att_src1'], 'L0_gnn_att_dst1': _L0_gnn_in['att_dst1'], 'L0_gnn_b1': _L0_gnn_in['b1'], 'L0_gnn_lW1': _L0_gnn_in['lW1'], 'L0_gnn_lb1': _L0_gnn_in['lb1'], 'L0_gnn_W2': _L0_gnn_in['W2'], 'L0_gnn_att_src2': _L0_gnn_in['att_src2'], 'L0_gnn_att_dst2': _L0_gnn_in['att_dst2'], 'L0_gnn_b2': _L0_gnn_in['b2'], 'L0_gnn_lW2': _L0_gnn_in['lW2'], 'L0_gnn_lb2': _L0_gnn_in['lb2'], 'L1_gnn_W_lin': _L1_gnn_in['W_lin'], 'L1_gnn_b_lin': _L1_gnn_in['b_lin'], 'L1_gnn_W_out': _L1_gnn_in['W_out'], 'L1_gnn_b_out': _L1_gnn_in['b_out']}

def reference(x, src, dst, L0_gnn_W1, L0_gnn_att_src1, L0_gnn_att_dst1, L0_gnn_b1, L0_gnn_lW1, L0_gnn_lb1, L0_gnn_W2, L0_gnn_att_src2, L0_gnn_att_dst2, L0_gnn_b2, L0_gnn_lW2, L0_gnn_lb2, L1_gnn_W_lin, L1_gnn_b_lin, L1_gnn_W_out, L1_gnn_b_out):
    import jax
    import jax.numpy as jnp

    def _L0_gnn_ref(x, edge_index, W1, att_src1, att_dst1, b1, lW1, lb1, W2, att_src2, att_dst2, b2, lW2, lb2):
        import jax, jax.numpy as jnp
        import numpy as np
        N, E, D, H = (6250, 100000, 64, 4)
        NEG_SLOPE = 0.2
        EPS = 1e-16

        def _gat(x, src, dst, W, att_src, att_dst, bias, n):
            xw = (x @ W).reshape(n, H, D)
            a_src = jnp.einsum('nhc,hc->nh', xw, att_src)
            a_dst = jnp.einsum('nhc,hc->nh', xw, att_dst)
            logits = jax.nn.leaky_relu(a_src[src] + a_dst[dst], NEG_SLOPE)
            m = jax.ops.segment_max(logits, dst, num_segments=n)
            ex = jnp.exp(logits - m[dst])
            s = jax.ops.segment_sum(ex, dst, num_segments=n)
            alpha = ex / (s[dst] + EPS)
            msg = xw[src] * alpha[..., None]
            out = jax.ops.segment_sum(msg, dst, num_segments=n)
            return out.mean(axis=1) + bias
        src, dst = (edge_index[0], edge_index[1])
        n = x.shape[0]
        h = _gat(x, src, dst, W1, att_src1, att_dst1, b1, n) + (x @ lW1 + lb1)
        h = jax.nn.relu(h)
        out = _gat(h, src, dst, W2, att_src2, att_dst2, b2, n) + (h @ lW2 + lb2)
        return out

    def _L1_gnn_ref(features, W_lin, b_lin, W_out, b_out, src, dst):
        import jax, jax.numpy as jnp
        import numpy as np
        N_NODES = 6250
        N_EDGES = 100000
        IN_C = 64
        n_nodes = features.shape[0]
        ef = jnp.concatenate([features[src], features[dst]], axis=-1)
        att = jax.nn.relu(ef @ W_lin.T + b_lin)
        mx = jax.ops.segment_max(att, dst, num_segments=n_nodes)
        ex = jnp.exp(att - mx[dst])
        den = jax.ops.segment_sum(ex, dst, num_segments=n_nodes)
        alpha = ex / den[dst]
        new_features = jax.ops.segment_sum(alpha * ef, dst, num_segments=n_nodes)
        return new_features @ W_out.T + b_out
    edge_index = jnp.stack([src, dst])
    x = _layernorm(x + _L0_gnn_ref(x, edge_index, L0_gnn_W1, L0_gnn_att_src1, L0_gnn_att_dst1, L0_gnn_b1, L0_gnn_lW1, L0_gnn_lb1, L0_gnn_W2, L0_gnn_att_src2, L0_gnn_att_dst2, L0_gnn_b2, L0_gnn_lW2, L0_gnn_lb2), axis=-1)
    x = _layernorm(x + _L1_gnn_ref(x, L1_gnn_W_lin, L1_gnn_b_lin, L1_gnn_W_out, L1_gnn_b_out, src, dst), axis=-1)
    return x

_drawn_inputs = setup_inputs


def setup_inputs(seed=0):
    import zlib

    import numpy as np

    out = dict(_drawn_inputs(seed))
    spreads = {'L0_gnn_b1': (0.0, 0.1),
     'L0_gnn_lb1': (0.0, 0.1),
     'L0_gnn_b2': (0.0, 0.1),
     'L0_gnn_lb2': (0.0, 0.1)}
    factors = {'L0_gnn_att_dst1': 2.94,
     'L0_gnn_att_dst2': 18.5,
     'L1_gnn_b_lin': 64.0,
     'L1_gnn_b_out': 7.598}
    for name, (base, spread) in spreads.items():
        noise = np.random.default_rng([zlib.crc32(name.encode()), seed]).standard_normal(out[name].shape)
        drawn = base * np.exp(spread * noise) if base else spread * noise
        out[name] = jnp.asarray(drawn.astype(out[name].dtype))
    for name, factor in factors.items():
        out[name] = (out[name] * factor).astype(out[name].dtype)
    return out
```

```python
import math
from contextlib import ExitStack, contextmanager

import concourse.bass as bass
from concourse import mybir

F32 = mybir.dt.float32
I32 = mybir.dt.int32
ALU = mybir.AluOpType
ACT = mybir.ActivationFunctionType
AX = mybir.AxisListType

P = 128


def slots_per_block(n_nodes, n_edges, n_blocks):
    mean = n_edges / n_nodes
    share = [math.exp(k * math.log(mean) - mean - math.lgamma(k + 1)) for k in range(int(8 * mean) + 64)]

    def largest(rank, spread):
        k = 0
        while True:
            above = n_nodes * sum(share[k + 1:])
            if above + spread * math.sqrt(above) <= rank:
                return max(k, 2)
            k += 1

    slots = [largest(max(P * b, 1e-4), 4.0 if b else 0.0) for b in range(n_blocks)]
    for b in range(2, n_blocks, 2):
        slots[b + 1] = slots[b]
    return slots


def runs_of_pairs(slots):
    runs, before = [], [0, 0]
    for u in range(len(slots) // 2):
        pair = slots[2 * u], slots[2 * u + 1]
        if u > 2 and runs[-1][2] == pair:
            runs[-1][1] += 1
        else:
            runs.append([u, 1, pair, tuple(before)])
        before = [before[0] + pair[0], before[1] + pair[1]]
    return runs


def landed_before(run, s, u):
    first, _, slots, before = run
    if s == 1:
        return landed(run, 0, u)
    return 16 * (slots[1] * (u - first) + before[1])


@contextmanager
def pairs_of(eng, run):
    first, count = run[0], run[1]
    if count == 1:
        yield first
    else:
        with eng.Fori(first, first + count) as u:
            yield u


def landed(run, s, u):
    first, _, slots, before = run
    return 16 * (slots[s] * (u - first) + before[s] + slots[s])


def build(nc, x, src, dst, W1, att_src1, att_dst1, b1, lW1, lb1, W2, att_src2, att_dst2, b2, lW2, lb2,
          W_lin, b_lin, W_out, b_out, out):
    N, D = x.shape
    E = src.shape[0]
    H = att_src1.shape[0]
    NB = -(-N // P)
    NP = NB * P
    assert NB % 14 == 0 and D == 64 and H == 4
    SLOTS = slots_per_block(N, E, NB)
    KMAX = SLOTS[0]
    RUNS = runs_of_pairs(SLOTS)
    assert RUNS[0][1] == RUNS[1][1] == 1
    SEG = max(k for k in range(1, int(math.isqrt(E)) + 1) if E % k == 0)
    NSEG = E // SEG
    CLS = KMAX + 1
    GROUPS = -(-(NB + 1) // 9)
    TW = D + 2 * H
    PLACE, NODE, START, DEGREE = range(TW, TW + 4)
    TX = TW + 4
    LW = 2 * D
    OW = TX + TW
    OWN = (0, TX, 0)
    NEG, LOW = -1e30, -1e29
    ALPHA_EPS, LN_EPS, SLOPE = 1e-16, 1e-5, 0.2
    FULL, REST = N // NB, N % NB

    ctx = ExitStack()
    with ctx:
        def sb(name, shape, dt=F32):
            return ctx.enter_context(nc.sbuf_tensor(name, shape, dt))

        def ps(name, shape):
            return ctx.enter_context(nc.psum_tensor(name, shape, F32))

        def sem(name):
            return ctx.enter_context(nc.semaphore(name))

        def scratch(name, shape, dt=F32):
            return nc.dram_tensor(name, shape, dt).ap()

        table1 = scratch("table1", [NP, TX])
        ordered = scratch("ordered", [NP, TX])
        place_of = scratch("place_of", [NP, 1], I32)
        table2 = scratch("table2", [NP, TW])
        table3 = scratch("table3", [NP, LW])
        src_padded = scratch("src_padded", [E + KMAX], I32)
        src_from = src_padded.rearrange("(a e) -> a e", a=1)

        half = 2 * KMAX * LW
        work = sb("work", [P, max(2 * half, NB * TX + 2 * CLS * NB + 14 * TX)])
        own = sb("own", [P, NB + 2, OW])
        idx_all = sb("idx_all", [P, NB + 1, KMAX], I32)
        rows_1 = work[:, 0:2 * KMAX * TX].rearrange("p (s k c) -> p s k c", s=2, k=KMAX)
        rows_2 = work[:, 0:2 * KMAX * TW].rearrange("p (s k c) -> p s k c", s=2, k=KMAX)
        rows_last = work[:, 0:half].rearrange("p (s k c) -> p s k c", s=2, k=KMAX)
        rows_of = (rows_1, rows_2, rows_last)
        weighted = work[:, half:2 * half]
        x_tab = work[:, 0:NB * TX].rearrange("p (b c) -> p b c", b=NB)
        at = NB * TX
        onehot = work[:, at:at + CLS * NB].rearrange("p (c b) -> p c b", c=CLS)
        onehot_flat = work[:, at:at + CLS * NB]
        prefix = work[:, at + CLS * NB:at + 2 * CLS * NB].rearrange("p (c b) -> p c b", c=CLS)
        prefix_flat = work[:, at + CLS * NB:at + 2 * CLS * NB]
        at += 2 * CLS * NB
        stage_e = work[:, at:at + 14 * TX].rearrange("p (j c) -> p j c", j=14)
        own_flat = own[:, :, :].rearrange("p b c -> p (b c)")
        segs = own_flat[:, 0:9 * SEG].bitcast(I32).rearrange("p (j e) -> p j e", j=9)

        below = own_flat[:, 9 * SEG:9 * SEG + 6 * NSEG].rearrange("p (j e) -> p j e", j=6)
        assert 9 * SEG + 6 * NSEG <= NB * OW

        ident = sb("ident", [P, P])
        before = sb("before", [P, P])
        ones = sb("ones", [P, P])
        slot_i = sb("slot_i", [P, KMAX], I32)
        slot_no = sb("slot_no", [P, KMAX])
        class_i = sb("class_i", [P, CLS], I32)
        class_no = sb("class_no", [P, CLS])
        node_i = sb("node_i", [P, 9 * GROUPS + 9], I32)
        node_no = sb("node_no", [P, 9 * GROUPS + 9])
        eps = sb("eps", [P, 1])
        zeros_i = sb("zeros_i", [1, KMAX], I32)
        last_i = sb("last_i", [1, NSEG], I32)
        last_f = sb("last_f", [1, NSEG])
        last_of_seg = sb("last_of_seg", [P, NSEG])
        seg_no = sb("seg_no", [P, 9 * GROUPS + 9])
        in_seg = sb("in_seg", [P, 9 * GROUPS])
        start = sb("start", [P, NB + 1])
        degree = sb("degree", [P, NB])
        capped = sb("capped", [P, NB])
        count = sb("count", [P, CLS])
        total = sb("total", [P, CLS])
        running = sb("running", [P, CLS])
        offset = sb("offset", [P, CLS])
        place = sb("place", [P, NB])
        place_i = sb("place_i", [P, NB], I32)
        place_lo = sb("place_lo", [P, NB], I32)
        place_hi = sb("place_hi", [P, NB], I32)
        order_at = sb("order_at", [P, NB], I32)
        deg = sb("deg", [P, NB])
        has_edge = sb("has_edge", [P, NB])
        start_of = sb("start_of", [P, NB])
        node_of = sb("node_of", [P, NB], I32)
        seg_now = sb("seg_now", [P, 9], I32)
        order_now = sb("order_now", [P, 14], I32)
        start_now = sb("start_now", [P, 2], I32)
        most_col = sb("most_col", [NB, 1])
        slots_row = sb("slots_row", [1, NB])
        most_row = sb("most_row", [1, NB])
        rounds_row = sb("rounds_row", [1, NB])
        rounds = sb("rounds", [1, NB], I32)
        most_rounds = sb("most_rounds", [1, 1], I32)
        heavy_at = sb("heavy_at", [P, 1])
        heavy_at_i = sb("heavy_at_i", [P, 1], I32)
        heavy_left = sb("heavy_left", [P, 1])
        heavy_top = sb("heavy_top", [P, D])
        heavy_den = sb("heavy_den", [P, D])
        heavy_part = sb("heavy_part", [P, D])
        w_in = [sb(f"w_in{l}", [D, H * D]) for l in (1, 2)]
        att_in = [[sb(f"att_in{l}{k}", [D, H * D]) for k in "sd"] for l in (1, 2)]
        att_prod = sb("att_prod", [D, H * D])
        w_coef = [sb(f"w_coef{l}", [D, 2 * H]) for l in (1, 2)]
        w_heads = [sb(f"w_heads{l}", [P, 2, D]) for l in (1, 2)]
        w_self = [sb(f"w_self{l}", [D + 1, D]) for l in (1, 2)]
        bias_b = sb("bias_b", [D + 1, 2, D])
        w_lin_in = sb("w_lin_in", [D, 2 * D])
        w_edge = sb("w_edge", [D + 1, 2 * D])
        w_out_in = sb("w_out_in", [D, 2 * D])
        w_out = sb("w_out", [2 * D, D])
        b_out_row = sb("b_out_row", [1, D])
        x7 = sb("x7", [P, 7, D])
        xT7 = sb("xT7", [D, 7 * P])
        own_now = sb("own_now", [P, 2, D])
        idx_now = sb("idx_now", [P, 2, KMAX], I32)
        node_now = sb("node_now", [P, 2], I32)
        idle = sb("idle", [P, KMAX])
        logit = sb("logit", [P, KMAX + 1, H])
        prob = sb("prob", [P, KMAX + 1, H])
        top = sb("top", [P, H])
        psum_ = sb("psum_", [P, H])
        scale = sb("scale", [P, H])
        sums = sb("sums", [P, 2, H * D])
        turned = sb("turned", [P, 2 * P])
        own_turned = sb("own_turned", [D + 1, P])
        row_turned = sb("row_turned", [D + 1, P])
        row = sb("row", [P, 2, LW])
        pre = sb("pre", [P, 2, D])
        stat = sb("stat", [P, 6])
        mean_var = sb("mean_var", [P, 2, 2])
        std = sb("std", [P, 2])
        inv_std = sb("inv_std", [P, 1])
        top_c = sb("top_c", [P, D])
        den_c = sb("den_c", [P, D])
        num_c = sb("num_c", [P, D])

        bank_v = ps("bank_v", [P, 512])
        bank_o = [ps("bank_o0", [P, 512]), ps("bank_o1", [P, 512])]
        bank_h = ps("bank_h", [P, 512])
        bank_a = ps("bank_a", [P, 512])
        bank_t = ps("bank_t", [P, 1024])
        bank_s = ps("bank_s", [P, 512])

        pool_go, dve_go, pe_go, sp_go = sem("pool_go"), sem("dve_go"), sem("pe_go"), sem("sp_go")
        consts_ready = sem("consts_ready")
        pool_zeroed = sem("pool_zeroed")
        x_zeroed = sem("x_zeroed")
        x_in = sem("x_in")
        last_in = sem("last_in")
        src_copied = sem("src_copied")
        weights_in = sem("weights_in")
        last_cast = sem("last_cast")
        last_spread = sem("last_spread")
        prep_step = sem("prep_step")
        weights_ready = sem("weights_ready")
        lin_turned = sem("lin_turned")
        x_staged = sem("x_staged")
        x_turned = sem("x_turned")
        x_turned_copied = sem("x_turned_copied")
        coef_made = sem("coef_made")
        coef_stored = sem("coef_stored")
        table1_out = sem("table1_out")
        seg_counted = sem("seg_counted")
        seg_staged = [sem(f"seg_staged{k}") for k in range(3)]
        seg_in = [sem(f"seg_in{k}") for k in range(3)]
        seg_scanned = sem("seg_scanned")
        counts_ready = sem("counts_ready")
        counts_summed = sem("counts_summed")
        places_ready = sem("places_ready")
        entry_staged = [sem(f"entry_staged{k}") for k in range(2)]
        entry_out = [sem(f"entry_out{k}") for k in range(2)]
        place_out = sem("place_out")
        own_in = [sem(f"own_in{k}") for k in range(2)]
        own_padded = sem("own_padded")
        idx_zeroed = sem("idx_zeroed")
        degs_ready = sem("degs_ready")
        degs_turned = sem("degs_turned")
        most_found = sem("most_found")
        most_turned = sem("most_turned")
        rounds_step = sem("rounds_step")
        rounds_ready = sem("rounds_ready")

        def per_pass(name, passes=(0, 1, 2)):
            return {p: sem(f"{name}_{p}") for p in passes}

        def per_pass_and_parity(name, passes=(0, 1, 2)):
            return {p: [sem(f"{name}_{p}{s}") for s in range(2)] for p in passes}

        idx_ready = per_pass_and_parity("idx_ready", (1, 2))
        start_staged = [sem(f"start_staged{s}") for s in range(2)]
        idx_in = [sem(f"idx_in{s}") for s in range(2)]
        places_kept = [sem(f"places_kept{s}") for s in range(2)]
        rows_in = per_pass_and_parity("rows_in")
        rows_used = per_pass_and_parity("rows_used")
        front_step = per_pass("front_step")
        logits_ready = per_pass("logits_ready")
        probs_ready = per_pass("probs_ready")
        sum_step = per_pass("sum_step")
        sums_ready = per_pass("sums_ready")
        own_staged = per_pass("own_staged", (0, 1))
        sums_turned = per_pass("sums_turned")
        turned_copied = per_pass("turned_copied")
        mixed = per_pass("mixed")
        mixed_read = per_pass("mixed_read")
        stat_step = per_pass("stat_step", (1, 2))
        stats_ready = per_pass("stats_ready", (1, 2))
        std_ready = per_pass("std_ready", (1, 2))
        norm_step = per_pass("norm_step", (1, 2))
        normed = per_pass("normed", (1, 2))
        row_in_pe = per_pass("row_in_pe", (0, 1))
        row_copied = per_pass("row_copied", (0, 1))
        extra_made = per_pass("extra_made", (0, 1))
        row_ready = per_pass("row_ready")
        own_ready = per_pass("own_ready", (0, 1))
        row_out = per_pass_and_parity("row_out")
        heavy_own = sem("heavy_own")
        heavy_init = per_pass("heavy_init")
        heavy_staged = sem("heavy_staged")
        heavy_idx = sem("heavy_idx")
        heavy_place = sem("heavy_place")
        heavy_rows = sem("heavy_rows")
        heavy_arrived = sem("heavy_arrived")
        heavy_step = sem("heavy_step")
        heavy_logits = sem("heavy_logits")
        heavy_probs = sem("heavy_probs")
        heavy_sum = sem("heavy_sum")
        heavy_end = per_pass("heavy_end")
        heavy_out = per_pass("heavy_out")

        N_WEIGHT_LOADS = 2 * (1 + 2 + H + 3) + 4

        def one(ap):
            return ap.rearrange("p a c -> p (a c)")

        ctx.enter_context(nc.allow_non_contiguous_dma(reason="the last edge of each segment"))
        block = ctx.enter_context(nc.Block())

        @block.sync
        def _(sp):
            sp.dma_start(last_i[:, :], dst.rearrange("(s e) -> s e", e=SEG)[:, SEG - 1:SEG]
                         .rearrange("s e -> e s")).then_inc(last_in, 16)
            sp.wait_ge(x_zeroed, 1)
            sp.dma_start(x_tab[0:FULL, :, 0:D], x[0:FULL * NB, :].rearrange("(p b) c -> p b c", b=NB))\
                .then_inc(x_in, 16)
            sp.dma_start(x_tab[FULL:FULL + 1, 0:REST, 0:D],
                         x[FULL * NB:N, :].rearrange("(p b) c -> p b c", p=1)).then_inc(x_in, 16)
            layers = ((W1, att_src1, att_dst1, b1, lW1, lb1), (W2, att_src2, att_dst2, b2, lW2, lb2))
            for l, (W, a_s, a_d, b, lW, lb) in enumerate(layers):
                sp.dma_start(w_in[l][:, :], W).then_inc(weights_in, 16)
                for k, a in enumerate((a_s, a_d)):
                    sp.dma_start(att_in[l][k][:, :], a.rearrange("h c -> (h c)").partition_broadcast(D))\
                        .then_inc(weights_in, 16)
                for h in range(H):
                    sp.dma_start(w_heads[l][D * (h % 2):D * (h % 2) + D, h // 2, :], W[:, D * h:D * h + D])\
                        .then_inc(weights_in, 16)
                sp.dma_start(w_self[l][0:D, :], lW).then_inc(weights_in, 16)
                sp.dma_start(bias_b[D:D + 1, l, :], b.rearrange("(a c) -> a c", a=1)).then_inc(weights_in, 16)
                sp.dma_start(w_self[l][D:D + 1, :], lb.rearrange("(a c) -> a c", a=1)).then_inc(weights_in, 16)
            sp.dma_start(w_lin_in[:, :], W_lin[0:D, :]).then_inc(weights_in, 16)
            sp.dma_start(w_edge[D:D + 1, D:2 * D], b_lin[0:D].rearrange("(a c) -> a c", a=1))\
                .then_inc(weights_in, 16)
            sp.dma_start(w_out_in[:, :], W_out).then_inc(weights_in, 16)
            sp.dma_start(b_out_row[:, :], b_out.rearrange("(a c) -> a c", a=1)).then_inc(weights_in, 16)
            sp.wait_ge(pool_zeroed, 1)
            sp.dma_start(src_padded[0:E].rearrange("(q e) -> q e", e=SEG),
                         src.rearrange("(q e) -> q e", e=SEG)).then_inc(src_copied, 16)
            sp.dma_start(src_padded[E:E + KMAX].rearrange("(a e) -> a e", a=1), zeros_i[:, :])\
                .then_inc(src_copied, 16)
            sp.wait_ge(coef_stored, NB // 7)
            sp.wait_ge(places_ready, 5)
            sp.dma_start(table1.rearrange("(p b) c -> p b c", b=NB), x_tab).then_inc(table1_out, 16)
            sp.dma_start(place_of.rearrange("(p b) a -> p (b a)", b=NB), place_i[:, :]).then_inc(place_out, 16)
            for k in range(2):
                sp.wait_ge(entry_out[k], 16 * 7 * (NB // 14))
            sp.wait_ge(seg_scanned, NB + 1 + 3)
            by_place = ordered.rearrange("(p b) c -> p b c", b=NB)
            for k, (b0, b1_) in enumerate(((0, 14), (14, NB))):
                sp.dma_start(own[:, b0:b1_, 0:TX], by_place[:, b0:b1_, :]).then_inc(own_in[k], 16)

            for p, (table, width) in enumerate(((table2, TW), (table3, LW))):
                with sp.Fori(0, NB // 2) as u:
                    for s in range(2):
                        sp.wait_ge(row_ready[p], 2 * u + s + 1)
                        sp.sem_inc(sp_go, 1)
                        sp.dma_start(table[bass.ds((2 * u + s) * P, P), :], row[:, s, 0:width])\
                            .then_inc(row_out[p][s], 16)
                for s in range(2):
                    sp.wait_ge(row_out[p][s], 16 * (NB // 2))
                sp.wait_ge(rounds_ready, 1)
                with sp.If(sp.value_load(most_rounds[0:1, 0:1], min_val=0, max_val=E) > 0):
                    done = sp.alloc_register(f"sp_done{p}")
                    sp.reg_mov(done, 0)
                    with sp.Fori(0, NB) as b:
                        with sp.If(sp.value_load(rounds[0:1, bass.ds(b, 1)], min_val=0, max_val=E) > 0):
                            h = sp.snap(done, min_val=0, max_val=NB)
                            sp.wait_ge(row_ready[p], h + NB + 1)
                            sp.sem_inc(sp_go, 1)
                            sp.dma_start(table[bass.ds(b * P, P), :], row[:, 0, 0:width]).then_inc(heavy_out[p], 16)
                            sp.wait_ge(heavy_out[p], 16 * h + 16)
                            sp.sem_inc(sp_go, 1)
                            sp.reg_add(done, done, 1)

        @block.gpsimd
        def _(pool):
            nc.gpsimd.memset(zeros_i[:, :], 0).then_inc(pool_zeroed, 1)
            nc.gpsimd.iota(node_i[:, :], [[1, 9 * GROUPS + 9]], base=0, channel_multiplier=NB).then_inc(consts_ready, 1)
            nc.gpsimd.memset(ident[:, :], 0.0).then_inc(consts_ready, 1)
            nc.gpsimd.memset(before[:, :], 1.0).then_inc(consts_ready, 1)
            nc.gpsimd.memset(ones[:, :], 1.0).then_inc(consts_ready, 1)
            nc.gpsimd.iota(slot_i[:, :], [[1, KMAX]], base=0, channel_multiplier=0).then_inc(consts_ready, 1)
            nc.gpsimd.iota(class_i[:, :], [[-1, CLS]], base=CLS - 1, channel_multiplier=0).then_inc(consts_ready, 1)
            pool.wait_ge(consts_ready, 6)
            nc.gpsimd.affine_select(out=ident[:, :], in_=ident[:, :], compare_op=ALU.not_equal, fill=1.0,
                                    base=0, pattern=[[-1, P]], channel_multiplier=1).then_inc(consts_ready, 1)
            nc.gpsimd.affine_select(out=before[:, :], in_=before[:, :], compare_op=ALU.is_gt, fill=0.0,
                                    base=0, pattern=[[1, P]], channel_multiplier=-1).then_inc(consts_ready, 1)

            seg_rows = dst.rearrange("(s e) -> s e", e=SEG)
            with pool.Fori(0, GROUPS) as j:
                for k in range(3):
                    pool.wait_ge(seg_staged[k], j + 1)
                    pool.sem_inc(pool_go, 1)
                    for c in range(3 * k, 3 * k + 3):
                        nc.gpsimd.indirect_dma_start(
                            segs[:, c, :], None, seg_rows,
                            bass.IndirectOffsetOnAxis(ap=seg_now[:, c:c + 1], axis=0)).then_inc(seg_in[k], 16)

            with pool.Fori(0, NB // 14) as j:
                for k in range(2):
                    pool.wait_ge(entry_staged[k], 2 * j + 2)
                    pool.sem_inc(pool_go, 1)
                    for c in range(7 * k, 7 * k + 7):
                        nc.gpsimd.indirect_dma_start(
                            ordered, bass.IndirectOffsetOnAxis(ap=order_now[:, c:c + 1], axis=0),
                            stage_e[:, c, :], None).then_inc(entry_out[k], 16)

            def gather(p, table, s, k):
                nc.gpsimd.indirect_dma_start(rows_of[p][:, s, k, :], None, table,
                                             bass.IndirectOffsetOnAxis(ap=idx_now[:, s, k:k + 1], axis=0))\
                    .then_inc(rows_in[p][s], 16)

            def fetch_sources(s):
                nc.gpsimd.indirect_dma_start(idx_now[:, s, :], None, src_from,
                                             bass.IndirectOffsetOnAxis(ap=start_now[:, s:s + 1], axis=1))\
                    .then_inc(idx_in[s], 16)

            def scatter(n, s, written):
                pool.wait_ge(row_ready[2], n + 1)
                pool.sem_inc(pool_go, 1)
                nc.gpsimd.indirect_dma_start(out, bass.IndirectOffsetOnAxis(ap=node_now[:, s:s + 1], axis=0),
                                             row[:, s, 0:D], None, bounds_check=N - 1, oob_is_err=False)\
                    .then_inc(written, 16)

            turn = pool.alloc_register("pool_turn")
            pool.reg_mov(turn, 0)

            def take_back(semaphore, count):
                nc.gpsimd.inc_swdge_sem([semaphore], [count], mode="sub")

            def heavy_gathers(p, table):
                with pool.If(pool.value_load(most_rounds[0:1, 0:1], min_val=0, max_val=E) > 0):
                    done = pool.alloc_register(f"pool_done{p}")
                    pool.reg_mov(done, 0)
                    with pool.Fori(0, NB) as b:
                        n_rounds = pool.value_load(rounds[0:1, bass.ds(b, 1)], min_val=0, max_val=E)
                        with pool.If(n_rounds > 0):
                            h = pool.snap(done, min_val=0, max_val=NB)
                            if p == 1:
                                first = nc.gpsimd.dma_start(
                                    own[:, bass.ds(b, 1), 0:TX],
                                    ordered.rearrange("(p b) c -> p b c", b=NB)[:, bass.ds(b, 1), :])
                                first.then_inc(heavy_own, 16)
                                nc.gpsimd.dma_start(own[:, bass.ds(b, 1), TX:OW].rearrange("p a c -> p (a c)"),
                                                    table2[bass.ds(b * P, P), :]).then_inc(heavy_own, 16)
                            with pool.Fori(0, n_rounds) as r:
                                g = pool.snap(turn, min_val=0, max_val=3 * E)
                                pool.wait_ge(heavy_staged, g + 1)
                                pool.sem_inc(pool_go, 1)
                                nc.gpsimd.indirect_dma_start(
                                    idx_now[:, 0, :], None, src_from,
                                    bass.IndirectOffsetOnAxis(ap=heavy_at_i[:, 0:1], axis=1)).then_inc(heavy_idx, 16)
                                pool.wait_ge(heavy_idx, 16)
                                take_back(heavy_idx, 16)
                                if p > 0:
                                    for k in range(KMAX):
                                        nc.gpsimd.indirect_dma_start(
                                            idx_now[:, 1, k:k + 1], None, place_of,
                                            bass.IndirectOffsetOnAxis(ap=idx_now[:, 0, k:k + 1], axis=0))\
                                            .then_inc(heavy_place, 16)
                                    pool.wait_ge(heavy_place, 16 * KMAX)
                                    take_back(heavy_place, 16 * KMAX)
                                for k in range(KMAX):
                                    nc.gpsimd.indirect_dma_start(
                                        rows_of[p][:, 0, k, :], None, table,
                                        bass.IndirectOffsetOnAxis(ap=idx_now[:, min(p, 1), k:k + 1], axis=0))\
                                        .then_inc(heavy_rows, 16)
                                pool.wait_ge(heavy_rows, 16 * KMAX)
                                take_back(heavy_rows, 16 * KMAX)
                                pool.sem_inc(heavy_arrived, 1)
                                pool.reg_add(turn, turn, 1)
                            if p == 2:
                                scatter(h + NB, 0, heavy_out[2])
                            pool.wait_ge(heavy_out[p], 16 * h + 16)
                            pool.reg_add(done, done, 1)

            for p, table in enumerate((table1, table2, table3)):
                if p == 0:
                    pool.wait_ge(src_copied, 32)
                    pool.wait_ge(table1_out, 16)
                    pool.wait_ge(start_staged[0], 1)
                    fetch_sources(0)
                else:
                    for s in range(2):
                        pool.wait_ge(row_out[p - 1][s], 16 * (NB // 2))
                        pool.wait_ge(rows_used[p - 1][s], NB // 2)
                for run in RUNS:
                    with pairs_of(pool, run) as u:
                        for s in range(2):
                            b, K = 2 * u + s, run[2][s]
                            if p == 0:
                                pool.wait_ge(idx_in[s], 16 * u + 16)
                            else:
                                pool.wait_ge(idx_ready[p][s], u + 1)
                            if run[0] > 0:
                                pool.wait_ge(rows_used[p][s], u)
                                if p == 0:
                                    pool.wait_ge(places_kept[s], u)
                            pool.sem_inc(pool_go, 1)
                            for k in range(K // 2 if p == 0 else K):
                                gather(p, table, s, k)
                            if p == 0:
                                pool.wait_ge(start_staged[1 - s], u + s + 1)
                                if run[0] > 0 or s == 1:
                                    pool.wait_ge(rows_in[0][1 - s], landed_before(run, s, u))
                                pool.sem_inc(pool_go, 1)
                                fetch_sources(1 - s)
                                for k in range(K // 2, K):
                                    gather(p, table, s, k)
                            if p == 2 and (run[0] > 1 or (run[0] == 1 and s == 1)):
                                scatter(b - 3, 1 - s, row_out[2][1 - s])
                if p == 2:
                    for b in range(NB - 3, NB):
                        scatter(b, b % 2, row_out[2][b % 2])
                for s in range(2):
                    pool.wait_ge(row_out[p][s], 16 * (NB // 2))
                if p == 0:
                    pool.wait_ge(place_out, 16)
                    pool.wait_ge(idx_in[0], 16 * (NB // 2) + 16)
                    pool.wait_ge(rounds_ready, 1)
                heavy_gathers(p, table)

        @block.vector
        def _(dve):
            nc.vector.memset(x_tab[96:P, :, :], 0.0).then_inc(x_zeroed, 1)
            nc.vector.memset(eps[:, :], LN_EPS).then_inc(prep_step, 1)
            nc.vector.memset(idx_all[:, :, :], 0).then_inc(prep_step, 1)
            nc.vector.memset(own_turned[D:D + 1, :], 1.0).then_inc(prep_step, 1)
            nc.vector.memset(row_turned[D:D + 1, :], 1.0).then_inc(prep_step, 1)
            nc.vector.memset(w_edge[D:D + 1, 0:D], 0.0).then_inc(prep_step, 1)
            for run in RUNS:
                b0 = 2 * run[0]
                for s in range(2 if run[0] == 0 else 1):
                    last = nc.vector.memset(slots_row[0:1, b0 + s:b0 + 2 * run[1]], float(run[2][s]))
                    if run[0] == 0 and s == 0:
                        last.then_inc(rounds_step, 1)
                        dve.wait_ge(rounds_step, 1)
            last.then_inc(prep_step, 1)

            dve.wait_ge(last_in, 16)
            nc.vector.tensor_copy(last_f[:, :], last_i[:, :]).then_inc(last_cast, 1)
            dve.wait_ge(consts_ready, 8)
            nc.vector.tensor_copy(node_no[:, :], node_i[:, :]).then_inc(prep_step, 1)
            nc.vector.tensor_copy(slot_no[:, :], slot_i[:, :]).then_inc(prep_step, 1)
            nc.vector.tensor_copy(class_no[:, :], class_i[:, :]).then_inc(prep_step, 1)
            dve.wait_ge(last_spread, 1)
            nc.vector.tensor_copy(last_of_seg[:, :], bank_s[:, 0:NSEG]).then_inc(prep_step, 1)
            dve.wait_ge(prep_step, 10)
            def count_segments(j, k):
                for c in range(3 * k, 3 * k + 3):
                    n = 9 * j + c
                    dve.wait_ge(seg_counted, n + 1)
                    nc.vector.tensor_scalar(below[:, c % 3, 0:NSEG], last_of_seg[:, :], node_no[:, bass.ds(n, 1)],
                                            None, ALU.is_lt, ALU.add, accum_out=seg_no[:, bass.ds(n, 1)])\
                        .then_inc(seg_counted, 1)

            def stage_segments(j, k):
                dve.wait_ge(seg_counted, 9 * j + 3 * k + 6)
                nc.vector.tensor_scalar(seg_now[:, 3 * k:3 * k + 3], seg_no[:, bass.ds(9 * j + 3 * k, 3)],
                                        float(NSEG - 1), None, ALU.min).then_inc(seg_staged[k], 1)

            dve.sem_inc(seg_counted, 3)
            dve.sem_inc(seg_scanned, 3)
            for k in range(3):
                count_segments(0, k)
                stage_segments(0, k)
            dve.wait_ge(weights_in, 16 * N_WEIGHT_LOADS)
            n_w = 0
            for l in range(2):
                for k in range(2):
                    if n_w:
                        dve.wait_ge(weights_ready, n_w)
                    nc.vector.tensor_tensor(att_prod[:, :], w_in[l][:, :], att_in[l][k][:, :], ALU.mult)\
                        .then_inc(weights_ready, 1)
                    dve.wait_ge(weights_ready, n_w + 1)
                    nc.vector.tensor_reduce(w_coef[l][:, H * k:H * k + H],
                                            att_prod[:, :].rearrange("p (h c) -> p h c", h=H), AX.X, ALU.add)\
                        .then_inc(weights_ready, 1)
                    n_w += 2
                nc.vector.tensor_tensor(w_self[l][D:D + 1, :], w_self[l][D:D + 1, :], bias_b[D:D + 1, l, :],
                                        ALU.add).then_inc(weights_ready, 1)
                n_w += 1
            dve.wait_ge(lin_turned, 1)
            nc.vector.tensor_copy(w_edge[0:D, :], bank_h[0:D, 0:2 * D]).then_inc(weights_ready, 1)
            nc.vector.tensor_copy(w_out[:, :], bank_h[:, 2 * D:3 * D]).then_inc(weights_ready, 1)

            with dve.Fori(0, GROUPS) as j:
                for k in range(3):
                    count_segments(j + 1, k)
                    dve.wait_ge(seg_in[k], 48 * j + 48)
                    for c in range(3 * k, 3 * k + 3):
                        n = 9 * j + c
                        dve.wait_ge(seg_scanned, n + 1)
                        nc.vector.tensor_scalar(below[:, 3 + c % 3, 0:SEG], segs[:, c, :], node_no[:, bass.ds(n, 1)],
                                                None, ALU.is_lt, ALU.add, accum_out=in_seg[:, bass.ds(n, 1)])\
                            .then_inc(seg_scanned, 1)
                    dve.wait_ge(seg_scanned, 9 * j + 3 * k + 6)
                    stage_segments(j + 1, k)
            dve.wait_ge(seg_counted, 9 * GROUPS + 9 + 3)
            nc.vector.tensor_scalar(seg_no[:, 0:NB + 1], seg_no[:, 0:NB + 1], float(NSEG - 1), None, ALU.min)\
                .then_inc(prep_step, 1)

            s0 = 11
            dve.wait_ge(prep_step, s0)
            nc.vector.scalar_tensor_tensor(out=start[:, :], in0=seg_no[:, 0:NB + 1], scalar=float(SEG),
                                           in1=in_seg[:, 0:NB + 1],
                                           op0=ALU.mult, op1=ALU.add).then_inc(prep_step, 1)
            dve.wait_ge(prep_step, s0 + 1)
            nc.vector.tensor_tensor(degree[:, :], start[:, 1:NB + 1], start[:, 0:NB], ALU.subtract)\
                .then_inc(prep_step, 1)
            dve.wait_ge(prep_step, s0 + 2)
            dve.wait_ge(x_zeroed, 1)
            nc.vector.tensor_copy(x_tab[:, :, NODE], node_no[:, 0:NB]).then_inc(places_ready, 1)
            nc.vector.tensor_copy(x_tab[:, :, START], start[:, 0:NB]).then_inc(places_ready, 1)
            nc.vector.tensor_copy(x_tab[:, :, DEGREE], degree[:, :]).then_inc(places_ready, 1)
            nc.vector.tensor_scalar(capped[:, :], degree[:, :], float(CLS - 1), None, ALU.min).then_inc(prep_step, 1)
            dve.wait_ge(prep_step, s0 + 3)
            nc.vector.tensor_tensor(onehot, capped[:, :].unsqueeze(1).to_broadcast([P, CLS, NB]),
                                    class_no[:, :].unsqueeze(2).to_broadcast([P, CLS, NB]), ALU.is_equal)\
                .then_inc(prep_step, 1)
            dve.wait_ge(prep_step, s0 + 4)
            nc.vector.tensor_reduce(count[:, :], onehot, AX.X, ALU.add).then_inc(counts_ready, 1)
            nc.vector.tensor_tensor_scan(prefix_flat, onehot_flat, onehot_flat, 0.0, ALU.add, ALU.max)\
                .then_inc(prep_step, 1)
            dve.wait_ge(counts_summed, 1)
            nc.vector.tensor_copy(total[:, :], bank_s[:, CLS:2 * CLS]).then_inc(prep_step, 1)
            dve.wait_ge(prep_step, s0 + 6)
            nc.vector.tensor_tensor_scan(running[:, :], total[:, :], total[:, :], 0.0, ALU.add, ALU.max)\
                .then_inc(prep_step, 1)
            dve.wait_ge(prep_step, s0 + 7)
            nc.vector.tensor_tensor(offset[:, :], running[:, :], total[:, :], ALU.subtract).then_inc(prep_step, 1)
            dve.wait_ge(prep_step, s0 + 8)
            nc.vector.tensor_tensor(offset[:, :], offset[:, :], bank_s[:, 0:CLS], ALU.add).then_inc(prep_step, 1)
            dve.wait_ge(prep_step, s0 + 9)
            nc.vector.tensor_tensor(offset[:, :], offset[:, :], count[:, :], ALU.add).then_inc(prep_step, 1)
            dve.wait_ge(prep_step, s0 + 10)
            nc.vector.scalar_tensor_tensor(out=offset[:, :], in0=offset[:, :], scalar=-1.0,
                                           in1=prefix[:, :, NB - 1], op0=ALU.add, op1=ALU.subtract)\
                .then_inc(prep_step, 1)
            dve.wait_ge(prep_step, s0 + 11)
            nc.vector.tensor_tensor(prefix, prefix, offset[:, :].unsqueeze(2).to_broadcast([P, CLS, NB]), ALU.add)\
                .then_inc(prep_step, 1)
            dve.wait_ge(prep_step, s0 + 12)
            nc.vector.tensor_tensor(prefix, prefix, onehot, ALU.mult).then_inc(prep_step, 1)
            dve.wait_ge(prep_step, s0 + 13)
            nc.vector.tensor_reduce(place[:, :], prefix.rearrange("p c b -> p b c"), AX.X, ALU.add)\
                .then_inc(prep_step, 1)
            dve.wait_ge(prep_step, s0 + 14)
            nc.vector.tensor_copy(place_i[:, :], place[:, :]).then_inc(prep_step, 1)
            nc.vector.tensor_copy(x_tab[:, :, PLACE], place[:, :]).then_inc(places_ready, 1)
            dve.wait_ge(prep_step, s0 + 15)
            nc.vector.tensor_single_scalar(place_lo[:, :], place_i[:, :], P - 1, ALU.bitwise_and).then_inc(prep_step, 1)
            nc.vector.tensor_single_scalar(place_hi[:, :], place_i[:, :], P.bit_length() - 1,
                                           ALU.logical_shift_right).then_inc(prep_step, 1)
            dve.wait_ge(prep_step, s0 + 17)
            nc.vector.scalar_tensor_tensor(out=order_at[:, :], in0=place_lo[:, :], scalar=float(NB),
                                           in1=place_hi[:, :], op0=ALU.mult, op1=ALU.add).then_inc(places_ready, 1)

            dve.wait_ge(seg_scanned, NB + 1 + 3)
            nc.vector.memset(own[:, NB:NB + 2, :], 0.0).then_inc(own_padded, 1)
            for k in range(2):
                dve.wait_ge(own_in[k], 16)
            nc.vector.tensor_copy(deg[:, :], own[:, 0:NB, DEGREE]).then_inc(degs_ready, 1)
            nc.vector.tensor_copy(start_of[:, :], own[:, 0:NB, START]).then_inc(degs_ready, 1)
            nc.vector.tensor_copy(node_of[:, :], own[:, 0:NB, NODE]).then_inc(degs_ready, 1)
            dve.wait_ge(degs_ready, 3)
            nc.vector.tensor_scalar(has_edge[:, :], deg[:, :], 1.0, None, ALU.min).then_inc(degs_ready, 1)
            dve.wait_ge(degs_turned, 1)
            nc.vector.tensor_reduce(most_col[:, :], bank_s[0:NB, 0:P], AX.X, ALU.max).then_inc(most_found, 1)
            dve.wait_ge(most_turned, 1)
            nc.vector.tensor_copy(most_row[:, :], bank_s[0:1, 0:NB]).then_inc(rounds_step, 1)
            dve.wait_ge(rounds_step, 2)
            nc.vector.tensor_tensor(slots_row[:, :], most_row[:, :], slots_row[:, :], ALU.is_gt)\
                .then_inc(rounds_step, 1)
            nc.vector.tensor_scalar(rounds_row[:, :], most_row[:, :], 1.0 / KMAX, 1.0, ALU.mult, ALU.add)\
                .then_inc(rounds_step, 1)
            dve.wait_ge(rounds_step, 4)
            nc.vector.tensor_tensor(rounds[:, :], rounds_row[:, :], slots_row[:, :], ALU.mult).then_inc(rounds_step, 1)
            dve.wait_ge(rounds_step, 5)
            nc.vector.tensor_reduce(most_rounds[:, :], rounds[:, :], AX.X, ALU.max).then_inc(rounds_ready, 1)
            dve.wait_ge(degs_ready, 4)

            def gat_front(p, b, s, K, arrived):
                n = 6 * b
                mine = own[:, bass.ds(b, 1), OWN[p] + D + H:OWN[p] + TW]
                lg, idl = logit[:, 0:K, :], idle[:, 0:K]
                dve.wait_ge(rows_in[p][s], arrived)
                nc.vector.tensor_tensor(lg, rows_of[p][:, s, 0:K, D:D + H], mine.to_broadcast([P, K, H]), ALU.add)\
                    .then_inc(front_step[p], 1)
                nc.vector.tensor_scalar(idl, slot_no[:, 0:K], deg[:, bass.ds(b, 1)], NEG, ALU.is_ge, ALU.mult)\
                    .then_inc(front_step[p], 1)
                dve.wait_ge(front_step[p], n + 1)
                nc.vector.scalar_tensor_tensor(out=lg, in0=lg, scalar=SLOPE, in1=lg, op0=ALU.mult, op1=ALU.max)\
                    .then_inc(front_step[p], 1)
                dve.wait_ge(front_step[p], n + 3)
                nc.vector.tensor_tensor(lg, lg, idl.unsqueeze(2).to_broadcast([P, K, H]), ALU.add)\
                    .then_inc(front_step[p], 1)
                dve.wait_ge(front_step[p], n + 4)
                nc.vector.tensor_reduce(top[:, :], lg.rearrange("p k h -> p h k"), AX.X, ALU.max)\
                    .then_inc(front_step[p], 1)
                dve.wait_ge(front_step[p], n + 5)
                nc.vector.tensor_scalar(top[:, :], top[:, :], LOW, None, ALU.max).then_inc(front_step[p], 1)
                dve.wait_ge(front_step[p], n + 6)
                nc.vector.tensor_tensor(lg, lg, top[:, :].unsqueeze(1).to_broadcast([P, K, H]), ALU.subtract)\
                    .then_inc(logits_ready[p], 1)

            def gat_sums(p, b, s, K):
                n = 5 * b
                pr = prob[:, 0:K, :]
                prod = weighted[:, 0:H * K * D].rearrange("p (h k c) -> p h k c", h=H, k=K)
                dve.wait_ge(probs_ready[p], b + 1)
                nc.vector.tensor_reduce(psum_[:, :], pr.rearrange("p k h -> p h k"), AX.X, ALU.add)\
                    .then_inc(sum_step[p], 1)
                dve.wait_ge(sum_step[p], n + 1)
                nc.vector.tensor_scalar(psum_[:, :], psum_[:, :], ALPHA_EPS, float(H), ALU.add, ALU.mult)\
                    .then_inc(sum_step[p], 1)
                dve.wait_ge(sum_step[p], n + 2)
                nc.vector.reciprocal(scale[:, :], psum_[:, :]).then_inc(sum_step[p], 1)
                dve.wait_ge(sum_step[p], n + 3)
                nc.vector.tensor_tensor(pr, pr, scale[:, :].unsqueeze(1).to_broadcast([P, K, H]), ALU.mult)\
                    .then_inc(sum_step[p], 1)
                dve.wait_ge(sum_step[p], n + 4)
                if not (isinstance(b, int) and b == 0):
                    dve.wait_ge(sums_ready[p], b)
                nc.vector.tensor_tensor(
                    prod, rows_of[p][:, s, 0:K, 0:D].unsqueeze(1).to_broadcast([P, H, K, D]),
                    pr.rearrange("p k h -> p h k").unsqueeze(3).to_broadcast([P, H, K, D]), ALU.mult)\
                    .then_inc(sum_step[p], 1)
                dve.wait_ge(sum_step[p], n + 5)
                dve.sem_inc(rows_used[p][s], 1)
                if not (isinstance(b, int) and b < 2):
                    dve.wait_ge(sums_turned[p], b - 1)
                nc.vector.tensor_reduce(sums[:, s, :].rearrange("p (h c) -> p h c", h=H),
                                        prod.rearrange("p h k c -> p h c k"), AX.X, ALU.add)\
                    .then_inc(sums_ready[p], 1)

            def last_front(b, s, K, arrived):
                p, n = 2, 5 * b
                z = weighted[:, 0:K * D].rearrange("p (k c) -> p k c", k=K)
                idl = idle[:, 0:K]
                dve.wait_ge(rows_in[p][s], arrived)
                nc.vector.tensor_tensor(z, rows_last[:, s, 0:K, D:2 * D],
                                        own[:, bass.ds(b, 1), D:2 * D].to_broadcast([P, K, D]), ALU.add)\
                    .then_inc(front_step[p], 1)
                nc.vector.tensor_scalar(idl, slot_no[:, 0:K], deg[:, bass.ds(b, 1)], NEG, ALU.is_ge, ALU.mult)\
                    .then_inc(front_step[p], 1)
                dve.wait_ge(front_step[p], n + 2)
                nc.vector.scalar_tensor_tensor(out=z, in0=z, scalar=0.0, in1=idl.unsqueeze(2).to_broadcast([P, K, D]),
                                               op0=ALU.max, op1=ALU.add).then_inc(front_step[p], 1)
                dve.wait_ge(front_step[p], n + 3)
                nc.vector.tensor_reduce(top_c[:, :], z.rearrange("p k c -> p c k"), AX.X, ALU.max)\
                    .then_inc(front_step[p], 1)
                dve.wait_ge(front_step[p], n + 4)
                nc.vector.tensor_scalar(top_c[:, :], top_c[:, :], 0.0, None, ALU.max).then_inc(front_step[p], 1)
                dve.wait_ge(front_step[p], n + 5)
                nc.vector.tensor_tensor(z, z, top_c[:, :].unsqueeze(1).to_broadcast([P, K, D]), ALU.subtract)\
                    .then_inc(logits_ready[p], 1)

            def last_sums(b, s, K):
                p, n = 2, 5 * b
                z = weighted[:, 0:K * D].rearrange("p (k c) -> p k c", k=K)
                prod = weighted[:, KMAX * D:KMAX * D + K * D].rearrange("p (k c) -> p k c", k=K)
                dve.wait_ge(probs_ready[p], b + 1)
                nc.vector.tensor_reduce(den_c[:, :], z.rearrange("p k c -> p c k"), AX.X, ALU.add)\
                    .then_inc(sum_step[p], 1)
                nc.vector.tensor_tensor(prod, z, rows_last[:, s, 0:K, 0:D], ALU.mult).then_inc(sum_step[p], 1)
                dve.wait_ge(sum_step[p], n + 2)
                dve.sem_inc(rows_used[p][s], 1)
                nc.vector.tensor_scalar(den_c[:, :], den_c[:, :], 0.5, None, ALU.max).then_inc(sum_step[p], 1)
                nc.vector.tensor_reduce(num_c[:, :], prod.rearrange("p k c -> p c k"), AX.X, ALU.add)\
                    .then_inc(sum_step[p], 1)
                dve.wait_ge(sum_step[p], n + 4)
                nc.vector.reciprocal(den_c[:, :], den_c[:, :]).then_inc(sum_step[p], 1)
                dve.wait_ge(sum_step[p], n + 5)
                if not (isinstance(b, int) and b < 2):
                    dve.wait_ge(sums_turned[p], b - 1)
                nc.vector.tensor_tensor(sums[:, s, 0:D], num_c[:, :], den_c[:, :], ALU.mult)\
                    .then_inc(sums_ready[p], 1)
                nc.vector.tensor_scalar(sums[:, s, D:2 * D], own[:, bass.ds(b, 1), 0:D].rearrange("p a c -> p (a c)"),
                                        has_edge[:, bass.ds(b, 1)], None, ALU.mult).then_inc(sums_ready[p], 1)

            def norm_stats(p, n, b, s):
                dve.wait_ge(mixed[p], n + 1)
                if not (isinstance(n, int) and n < 2):
                    dve.wait_ge(normed[p], n - 1)
                nc.vector.tensor_tensor(pre[:, s, :], bank_o[s][:, 0:D], one(own[:, bass.ds(b, 1), 0:D]), ALU.add)\
                    .then_inc(mixed_read[p], 1)
                dve.wait_ge(mixed_read[p], n + 1)
                nc.vector.bn_stats(stat[:, :], pre[:, s, :]).then_inc(stat_step[p], 1)
                dve.wait_ge(stat_step[p], n + 1)
                dve.sem_inc(dve_go, 1)
                nc.vector.bn_aggr(mean_var[:, s, :], stat[:, :]).then_inc(stats_ready[p], 1)

            def norm_row(p, n, s, written):
                dve.wait_ge(std_ready[p], n + 1)
                nc.vector.reciprocal(inv_std[:, :], std[:, s:s + 1]).then_inc(norm_step[p], 1)
                dve.wait_ge(norm_step[p], n + 1)
                if not (isinstance(written, int) and written == 0):
                    dve.wait_ge(row_out[p][s], 16 * written)
                nc.vector.tensor_scalar(row[:, s, 0:D], pre[:, s, :], mean_var[:, s, 0:1], inv_std[:, 0:1],
                                        ALU.subtract, ALU.mult).then_inc(normed[p], 1)

            turn = dve.alloc_register("dve_turn")
            dve.reg_mov(turn, 0)

            def heavy_round(p, b, g):
                C, n = (H, 10 * g) if p < 2 else (D, 10 * g)
                lg = logit[:, :, :] if p < 2 else weighted[:, 0:(KMAX + 1) * D].rearrange("p (k c) -> p k c", c=D)
                pr = prob[:, :, :] if p < 2 else lg
                lk = lg[:, 0:KMAX, :]
                rows = rows_of[p][:, 0, :, :]
                if p < 2:
                    theirs, mine = rows[:, :, D:D + H], own[:, bass.ds(b, 1), OWN[p] + D + H:OWN[p] + TW]
                else:
                    theirs, mine = rows[:, :, D:2 * D], own[:, bass.ds(b, 1), D:2 * D]
                nc.vector.tensor_copy(heavy_at_i[:, :], heavy_at[:, :]).then_inc(heavy_staged, 1)
                dve.wait_ge(heavy_arrived, g + 1)
                nc.vector.tensor_tensor(lk, theirs, mine.to_broadcast([P, KMAX, C]), ALU.add).then_inc(heavy_step, 1)
                nc.vector.tensor_scalar(idle[:, :], slot_no[:, :], heavy_left[:, 0:1], NEG, ALU.is_ge, ALU.mult)\
                    .then_inc(heavy_step, 1)
                dve.wait_ge(heavy_step, n + 2)
                idl = idle[:, :].unsqueeze(2).to_broadcast([P, KMAX, C])
                if p < 2:
                    nc.vector.scalar_tensor_tensor(out=lk, in0=lk, scalar=SLOPE, in1=lk, op0=ALU.mult, op1=ALU.max)\
                        .then_inc(heavy_step, 1)
                    dve.wait_ge(heavy_step, n + 3)
                    nc.vector.tensor_tensor(lk, lk, idl, ALU.add).then_inc(heavy_step, 1)
                else:
                    nc.vector.scalar_tensor_tensor(out=lk, in0=lk, scalar=0.0, in1=idl, op0=ALU.max, op1=ALU.add)\
                        .then_inc(heavy_step, 2)
                dve.wait_ge(heavy_step, n + 4)
                nc.vector.tensor_reduce(heavy_part[:, 0:C], lk.rearrange("p k c -> p c k"), AX.X, ALU.max)\
                    .then_inc(heavy_step, 1)
                dve.wait_ge(heavy_step, n + 5)
                nc.vector.tensor_tensor(heavy_part[:, 0:C], heavy_part[:, 0:C], heavy_top[:, 0:C], ALU.max)\
                    .then_inc(heavy_step, 1)
                dve.wait_ge(heavy_step, n + 6)
                nc.vector.tensor_tensor(lg[:, KMAX, :], heavy_top[:, 0:C], heavy_part[:, 0:C], ALU.subtract)\
                    .then_inc(heavy_step, 1)
                dve.wait_ge(heavy_step, n + 7)
                nc.vector.tensor_copy(heavy_top[:, 0:C], heavy_part[:, 0:C]).then_inc(heavy_step, 1)
                dve.wait_ge(heavy_step, n + 8)
                nc.vector.tensor_tensor(lk, lk, heavy_top[:, 0:C].unsqueeze(1).to_broadcast([P, KMAX, C]),
                                        ALU.subtract).then_inc(heavy_logits, 1)
                dve.wait_ge(heavy_probs, g + 1)
                k = pr[:, 0:KMAX, :]
                rose = pr[:, KMAX, :]
                m = 8 * g
                nc.vector.tensor_tensor(heavy_den[:, 0:C], heavy_den[:, 0:C], rose, ALU.mult).then_inc(heavy_sum, 1)
                nc.vector.tensor_reduce(heavy_part[:, 0:C], k.rearrange("p k c -> p c k"), AX.X, ALU.add)\
                    .then_inc(heavy_sum, 1)
                if p < 2:
                    acc = sums[:, 0, :].rearrange("p (h c) -> p h c", h=H)
                    rise = rose.unsqueeze(2).to_broadcast([P, H, D])
                    prod = weighted[:, 0:H * KMAX * D].rearrange("p (h k c) -> p h k c", h=H, k=KMAX)
                    nc.vector.tensor_tensor(prod, rows[:, :, 0:D].unsqueeze(1).to_broadcast([P, H, KMAX, D]),
                                            k.rearrange("p k h -> p h k").unsqueeze(3).to_broadcast([P, H, KMAX, D]),
                                            ALU.mult).then_inc(heavy_sum, 1)
                    more, parts = sums[:, 1, :].rearrange("p (h c) -> p h c", h=H), prod.rearrange("p h k c -> p h c k")
                else:
                    acc, rise = sums[:, 0, 0:D], rose
                    prod = weighted[:, (KMAX + 1) * D:(2 * KMAX + 1) * D].rearrange("p (k c) -> p k c", c=D)
                    nc.vector.tensor_tensor(prod, rows[:, :, 0:D], k, ALU.mult).then_inc(heavy_sum, 1)
                    more, parts = sums[:, 1, 0:D], prod.rearrange("p k c -> p c k")
                nc.vector.tensor_tensor(acc, acc, rise, ALU.mult).then_inc(heavy_sum, 1)
                dve.wait_ge(heavy_sum, m + 4)
                nc.vector.tensor_tensor(heavy_den[:, 0:C], heavy_den[:, 0:C], heavy_part[:, 0:C], ALU.add)\
                    .then_inc(heavy_sum, 1)
                nc.vector.tensor_reduce(more, parts, AX.X, ALU.add).then_inc(heavy_sum, 1)
                dve.wait_ge(heavy_sum, m + 6)
                nc.vector.tensor_tensor(acc, acc, more, ALU.add).then_inc(heavy_sum, 1)
                nc.vector.tensor_scalar(heavy_at[:, :], heavy_at[:, :], float(KMAX), float(E), ALU.add, ALU.min)\
                    .then_inc(heavy_step, 1)
                nc.vector.tensor_scalar(heavy_left[:, :], heavy_left[:, :], -float(KMAX), None, ALU.add)\
                    .then_inc(heavy_step, 1)
                dve.wait_ge(heavy_step, n + 10)
                dve.sem_inc(heavy_sum, 1)
                dve.wait_ge(heavy_sum, m + 8)

            def heavy_blocks(p):
                for s in range(2):
                    dve.wait_ge(row_out[p][s], 16 * (NB // 2))
                if p < 2:
                    dve.wait_ge(own_ready[p], (1 + p) * NB)
                with dve.If(dve.value_load(most_rounds[0:1, 0:1], min_val=0, max_val=E) > 0):
                    done = dve.alloc_register(f"dve_done{p}")
                    dve.reg_mov(done, 0)
                    with dve.Fori(0, NB) as b:
                        n_rounds = dve.value_load(rounds[0:1, bass.ds(b, 1)], min_val=0, max_val=E)
                        with dve.If(n_rounds > 0):
                            h = dve.snap(done, min_val=0, max_val=NB)
                            n = h + NB
                            nc.vector.tensor_copy(heavy_at[:, :], start_of[:, bass.ds(b, 1)]).then_inc(heavy_init[p], 1)
                            nc.vector.tensor_copy(heavy_left[:, :], deg[:, bass.ds(b, 1)]).then_inc(heavy_init[p], 1)
                            nc.vector.memset(heavy_top[:, :], LOW if p < 2 else 0.0).then_inc(heavy_init[p], 1)
                            nc.vector.memset(heavy_den[:, :], 0.0).then_inc(heavy_init[p], 1)
                            nc.vector.memset(sums[:, 0, :], 0.0).then_inc(heavy_init[p], 1)
                            dve.wait_ge(heavy_init[p], 5 * h + 5)
                            if p == 1:
                                dve.wait_ge(heavy_own, 32 * h + 32)
                            dve.sem_inc(dve_go, 1)
                            with dve.Fori(0, n_rounds) as r:
                                heavy_round(p, b, dve.snap(turn, min_val=0, max_val=3 * E))
                                dve.reg_add(turn, turn, 1)
                            e = 2 * h
                            if p < 2:
                                nc.vector.tensor_scalar(heavy_den[:, 0:H], heavy_den[:, 0:H], ALPHA_EPS, float(H),
                                                        ALU.add, ALU.mult).then_inc(heavy_end[p], 1)
                                dve.wait_ge(heavy_end[p], e + 1)
                                nc.vector.reciprocal(scale[:, :], heavy_den[:, 0:H]).then_inc(heavy_end[p], 1)
                                dve.wait_ge(heavy_end[p], e + 2)
                                acc = sums[:, 0, :].rearrange("p (h c) -> p h c", h=H)
                                nc.vector.tensor_tensor(acc, acc, scale[:, :].unsqueeze(2).to_broadcast([P, H, D]),
                                                        ALU.mult).then_inc(sums_ready[p], 1)
                            else:
                                nc.vector.tensor_scalar(heavy_den[:, :], heavy_den[:, :], 0.5, None, ALU.max)\
                                    .then_inc(heavy_end[p], 1)
                                dve.wait_ge(heavy_end[p], e + 1)
                                nc.vector.reciprocal(heavy_den[:, :], heavy_den[:, :]).then_inc(heavy_end[p], 1)
                                dve.wait_ge(heavy_end[p], e + 2)
                                nc.vector.tensor_tensor(sums[:, 0, 0:D], sums[:, 0, 0:D], heavy_den[:, :], ALU.mult)\
                                    .then_inc(sums_ready[p], 1)
                                nc.vector.tensor_scalar(sums[:, 0, D:2 * D], one(own[:, bass.ds(b, 1), 0:D]),
                                                        has_edge[:, bass.ds(b, 1)], None, ALU.mult)\
                                    .then_inc(sums_ready[p], 1)
                            if p > 0:
                                norm_stats(p, n, b, 0)
                                norm_row(p, n, 0, NB // 2)
                            dve.wait_ge(heavy_out[p], 16 * h + 16)
                            dve.reg_add(done, done, 1)

            for p in range(3):
                for run in RUNS:
                    with pairs_of(dve, run) as u:
                        for s in range(2):
                            b, K = 2 * u + s, run[2][s]
                            if p < 2:
                                gat_front(p, b, s, K, landed(run, s, u))
                            else:
                                last_front(b, s, K, landed(run, s, u))
                            if p > 0 and run[0] > 0:
                                norm_row(p, b - 2, s, u - 1)
                            if p < 2:
                                gat_sums(p, b, s, K)
                            else:
                                last_sums(b, s, K)
                            if p > 0 and (run[0] > 0 or s == 1):
                                norm_stats(p, b - 1, b - 1, 1 - s)
                if p > 0:
                    norm_row(p, NB - 2, 0, NB // 2 - 1)
                    norm_stats(p, NB - 1, NB - 1, 1)
                    norm_row(p, NB - 1, 1, NB // 2 - 1)
                heavy_blocks(p)

        @block.scalar
        def _(act):
            act.wait_ge(x_in, 32)
            with act.Fori(0, NB // 7) as j:
                nc.scalar.activation(x7[:, :, :], x_tab[:, bass.ds(7 * j, 7), 0:D], ACT.Copy).then_inc(x_staged, 1)
                act.wait_ge(x_turned, j + 1)
                nc.scalar.activation(xT7[:, :], bank_t[0:D, 0:7 * P], ACT.Copy).then_inc(x_turned_copied, 1)
                act.wait_ge(coef_made, j + 1)
                nc.scalar.activation(x_tab[:, bass.ds(7 * j, 7), D:TW],
                                     bank_a[:, 0:7 * 2 * H].rearrange("p (b c) -> p b c", b=7), ACT.Copy)\
                    .then_inc(coef_stored, 1)

            act.wait_ge(places_ready, 5)
            for k in range(2):
                nc.scalar.activation(order_now[:, 7 * k:7 * k + 7], order_at[:, 7 * k:7 * k + 7], ACT.Copy)\
                    .then_inc(entry_staged[k], 1)
                nc.scalar.activation(stage_e[:, 7 * k:7 * k + 7, :], x_tab[:, 7 * k:7 * k + 7, :], ACT.Copy)\
                    .then_inc(entry_staged[k], 1)
            with act.Fori(1, NB // 14) as j:
                for k in range(2):
                    act.wait_ge(entry_out[k], 112 * j)
                    nc.scalar.activation(order_now[:, 7 * k:7 * k + 7], order_at[:, bass.ds(14 * j + 7 * k, 7)],
                                         ACT.Copy).then_inc(entry_staged[k], 1)
                    nc.scalar.activation(stage_e[:, 7 * k:7 * k + 7, :], x_tab[:, bass.ds(14 * j + 7 * k, 7), :],
                                         ACT.Copy).then_inc(entry_staged[k], 1)

            def stage_sources(p, b, s):
                nc.scalar.activation(idx_now[:, s, :], idx_all[:, bass.ds(b, 1), :].rearrange("p a k -> p (a k)"),
                                     ACT.Copy).then_inc(idx_ready[p][s], 1)

            def stage_start(b, s):
                nc.scalar.activation(start_now[:, s:s + 1], own[:, bass.ds(b, 1), START], ACT.Copy)\
                    .then_inc(start_staged[s], 1)

            def keep_places(b, s, K):
                nc.scalar.activation(one(idx_all[:, bass.ds(b, 1), 0:K]), rows_1[:, s, 0:K, PLACE], ACT.Copy)\
                    .then_inc(places_kept[s], 1)

            def exponentials(p, b, K):
                act.wait_ge(logits_ready[p], b + 1)
                if p < 2:
                    nc.scalar.activation(prob[:, 0:K, :], logit[:, 0:K, :], ACT.Exp).then_inc(probs_ready[p], 1)
                else:
                    nc.scalar.activation(weighted[:, 0:K * D], weighted[:, 0:K * D], ACT.Exp)\
                        .then_inc(probs_ready[p], 1)

            def stage_own(p, n, b, s):
                if not (isinstance(n, int) and n < 2):
                    act.wait_ge(sums_turned[p], n - 1)
                nc.scalar.activation(own_now[:, s, :], one(own[:, bass.ds(b, 1), OWN[p]:OWN[p] + D]), ACT.Copy)\
                    .then_inc(own_staged[p], 1)

            def copy_turned(p, n):
                act.wait_ge(sums_turned[p], n + 1)
                if not (isinstance(n, int) and n == 0):
                    act.wait_ge(mixed[p], n)
                if p < 2:
                    nc.scalar.activation(turned[:, :], bank_v[:, 0:2 * P], ACT.Copy).then_inc(turned_copied[p], 1)
                    nc.scalar.activation(own_turned[0:D, :], bank_v[0:D, 2 * P:3 * P], ACT.Copy)\
                        .then_inc(turned_copied[p], 1)
                else:
                    nc.scalar.activation(turned[:, 0:P], bank_v[:, 0:P], ACT.Copy).then_inc(turned_copied[p], 2)

            def copy_row_turned(p, n):
                act.wait_ge(row_in_pe[p], n + 1)
                if not (isinstance(n, int) and n == 0):
                    act.wait_ge(extra_made[p], n)
                nc.scalar.activation(row_turned[0:D, :], bank_h[0:D, 0:P], ACT.Copy).then_inc(row_copied[p], 1)

            def gat1_row(n, b, s, written):
                act.wait_ge(mixed[0], n + 1)
                if not (isinstance(written, int) and written == 0):
                    act.wait_ge(row_out[0][s], 16 * written)
                nc.scalar.activation(row[:, s, 0:D], bank_o[s][:, 0:D], ACT.Relu).then_inc(mixed_read[0], 1)
                copy_row_turned(0, n)
                act.wait_ge(extra_made[0], n + 1)
                nc.scalar.activation(row[:, s, D:TW], bank_a[:, 0:2 * H], ACT.Copy).then_inc(row_ready[0], 1)
                act.wait_ge(row_ready[0], n + 1)
                nc.scalar.activation(one(own[:, bass.ds(b, 1), TX:OW]), row[:, s, 0:TW], ACT.Copy)\
                    .then_inc(own_ready[0], 1)

            def gat2_row(n, b, s):
                copy_row_turned(1, n)
                act.wait_ge(extra_made[1], n + 1)
                nc.scalar.activation(row[:, s, D:2 * D], bank_a[:, 0:D], ACT.Copy).then_inc(row_ready[1], 1)
                nc.scalar.activation(one(own[:, bass.ds(b, 1), D:2 * D]), bank_a[:, D:2 * D], ACT.Copy)\
                    .then_inc(own_ready[1], 1)
                nc.scalar.activation(one(own[:, bass.ds(b, 1), 0:D]), row[:, s, 0:D], ACT.Copy)\
                    .then_inc(own_ready[1], 1)

            def last_row(n, b, s):
                act.wait_ge(normed[2], n + 1)
                nc.scalar.activation(node_now[:, s:s + 1], node_of[:, bass.ds(b, 1)], ACT.Copy)\
                    .then_inc(row_ready[2], 1)

            def deviation(p, n, s):
                act.wait_ge(stats_ready[p], n + 1)
                nc.scalar.activation(std[:, s:s + 1], mean_var[:, s, 1:2], ACT.Sqrt, bias=eps[:, 0:1])\
                    .then_inc(std_ready[p], 1)

            def finish_row(p, n, b, s):
                if p == 1:
                    gat2_row(n, b, s)
                else:
                    last_row(n, b, s)

            def heavy_blocks(p):
                for s in range(2):
                    act.wait_ge(row_out[p][s], 16 * (NB // 2))
                with act.If(act.value_load(most_rounds[0:1, 0:1], min_val=0, max_val=E) > 0):
                    done = act.alloc_register(f"act_done{p}")
                    act.reg_mov(done, 0)
                    with act.Fori(0, NB) as b:
                        n_rounds = act.value_load(rounds[0:1, bass.ds(b, 1)], min_val=0, max_val=E)
                        with act.If(n_rounds > 0):
                            h = act.snap(done, min_val=0, max_val=NB)
                            n = h + NB
                            if p == 1:
                                act.wait_ge(heavy_own, 32 * h + 32)
                            if p < 2:
                                stage_own(p, n, b, 0)
                            with act.Fori(0, n_rounds) as r:
                                g = act.snap(turn, min_val=0, max_val=3 * E)
                                act.wait_ge(heavy_logits, g + 1)
                                if p < 2:
                                    nc.scalar.activation(prob[:, :, :], logit[:, :, :], ACT.Exp)\
                                        .then_inc(heavy_probs, 1)
                                else:
                                    nc.scalar.activation(weighted[:, 0:(KMAX + 1) * D], weighted[:, 0:(KMAX + 1) * D],
                                                         ACT.Exp).then_inc(heavy_probs, 1)
                                act.reg_add(turn, turn, 1)
                            copy_turned(p, n)
                            if p == 0:
                                gat1_row(n, b, 0, NB // 2)
                            else:
                                deviation(p, n, 0)
                                finish_row(p, n, b, 0)
                            act.wait_ge(heavy_out[p], 16 * h + 16)
                            act.reg_add(done, done, 1)

            turn = act.alloc_register("act_turn")
            act.reg_mov(turn, 0)
            act.wait_ge(own_in[0], 16)
            for b in range(2):
                stage_start(b, b)
            act.wait_ge(own_in[1], 16)
            act.wait_ge(own_padded, 1)
            act.wait_ge(prep_step, 6)
            act.wait_ge(degs_ready, 4)
            act.wait_ge(rounds_ready, 1)
            for p in range(3):
                if p > 0:
                    stage_sources(p, 0, 0)
                for run in RUNS:
                    with pairs_of(act, run) as u:
                        for s in range(2):
                            b, K = 2 * u + s, run[2][s]
                            if p == 0:
                                act.wait_ge(idx_in[s], 16 * u + 16)
                                stage_start(b + 2, s)
                            else:
                                if run[0] > 0 or s == 1:
                                    act.wait_ge(rows_in[p][1 - s], landed_before(run, s, u))
                                stage_sources(p, b + 1, 1 - s)
                            exponentials(p, b, K)
                            if p == 0:
                                keep_places(b, s, K)
                            if p < 2:
                                stage_own(p, b, b, s)
                            if run[0] > 0 or s == 1:
                                copy_turned(p, b - 1)
                                if p == 0:
                                    gat1_row(b - 1, b - 1, 1 - s, u - 1 + s)
                            if p > 0 and run[0] > 0:
                                finish_row(p, b - 2, b - 2, s)
                            if p > 0 and (run[0] > 0 or s == 1):
                                deviation(p, b - 1, 1 - s)
                copy_turned(p, NB - 1)
                if p == 0:
                    gat1_row(NB - 1, NB - 1, 1, NB // 2 - 1)
                    act.wait_ge(idx_in[0], 16 * (NB // 2) + 16)
                else:
                    finish_row(p, NB - 2, NB - 2, 0)
                    deviation(p, NB - 1, 1)
                    finish_row(p, NB - 1, NB - 1, 1)
                heavy_blocks(p)

        @block.tensor
        def _(pe):
            pe.wait_ge(consts_ready, 8)
            pe.wait_ge(last_cast, 1)
            nc.tensor.matmul(bank_s[:, 0:NSEG], ones[0:1, :], last_f[:, :], start=True, stop=True)\
                .then_inc(last_spread, 1)
            pe.wait_ge(weights_in, 16 * N_WEIGHT_LOADS)
            nc.tensor.transpose(bank_h[0:D, 0:D], w_lin_in[:, 0:D], ident[0:D, 0:D])
            nc.tensor.transpose(bank_h[0:D, D:2 * D], w_lin_in[:, D:2 * D], ident[0:D, 0:D])
            nc.tensor.transpose(bank_h[:, 2 * D:3 * D], w_out_in[:, :], ident[0:D, 0:D]).then_inc(lin_turned, 1)
            pe.wait_ge(weights_ready, 12)

            def turn_x(j):
                pe.wait_ge(x_staged, j + 1)
                pe.sem_inc(pe_go, 1)
                for c in range(7):
                    last = nc.tensor.transpose(bank_t[0:D, P * c:P * c + P],
                                               x7[:, c, :], ident[:, :])
                last.then_inc(x_turned, 1)

            def make_coef(j):
                pe.wait_ge(x_turned_copied, j + 1)
                for c in range(7):
                    last = nc.tensor.matmul(bank_a[:, 2 * H * c:2 * H * c + 2 * H], xT7[:, P * c:P * c + P],
                                            w_coef[0][:, :], start=True, stop=True)
                last.then_inc(coef_made, 1)

            turn_x(0)
            make_coef(0)
            with pe.Fori(1, NB // 7) as j:
                pe.wait_ge(x_turned_copied, j)
                turn_x(j)
                pe.wait_ge(coef_stored, j)
                make_coef(j)
            pe.wait_ge(counts_ready, 1)
            nc.tensor.matmul(bank_s[:, 0:CLS], before[:, :], count[:, :], start=True, stop=True)
            nc.tensor.matmul(bank_s[:, CLS:2 * CLS], ones[:, :], count[:, :], start=True, stop=True)\
                .then_inc(counts_summed, 1)

            pe.wait_ge(degs_ready, 4)
            nc.tensor.transpose(bank_s[0:NB, 0:P], deg[:, :], ident[:, :]).then_inc(degs_turned, 1)
            pe.wait_ge(most_found, 1)
            nc.tensor.transpose(bank_s[0:1, 0:NB], most_col[:, :], ident[0:NB, 0:NB]).then_inc(most_turned, 1)

            def turn_sums(p, b, s):
                if p < 2:
                    pe.wait_ge(sums_ready[p], b + 1)
                else:
                    pe.wait_ge(sums_ready[p], 2 * b + 2)
                if not (isinstance(b, int) and b == 0):
                    pe.wait_ge(turned_copied[p], 2 * b)
                pe.sem_inc(pe_go, 1)
                if p < 2:
                    nc.tensor.transpose(bank_v[:, 0:P], sums[:, s, 0:P], ident[:, :])
                    nc.tensor.transpose(bank_v[:, P:2 * P], sums[:, s, P:2 * P], ident[:, :])
                    pe.wait_ge(own_staged[p], b + 1)
                    pe.sem_inc(pe_go, 1)
                    nc.tensor.transpose(bank_v[0:D, 2 * P:3 * P], own_now[:, s, :], ident[:, :])\
                        .then_inc(sums_turned[p], 1)
                else:
                    nc.tensor.transpose(bank_v[:, 0:P], sums[:, s, 0:P], ident[:, :]).then_inc(sums_turned[p], 1)

            def mix(p, b, s):
                pe.wait_ge(turned_copied[p], 2 * b + 2)
                if not (isinstance(b, int) and b < 2):
                    pe.wait_ge(mixed_read[p], b - 1)
                o = bank_o[s][:, 0:D]
                if p < 2:
                    nc.tensor.matmul(o, turned[:, 0:P], w_heads[p][:, 0, :], start=True, stop=False)
                    nc.tensor.matmul(o, turned[:, P:2 * P], w_heads[p][:, 1, :], start=False, stop=False)
                    nc.tensor.matmul(o, own_turned[:, :], w_self[p][:, :], start=False, stop=True)\
                        .then_inc(mixed[p], 1)
                else:
                    nc.tensor.matmul(o, turned[:, 0:P], w_out[:, :], start=True, stop=False)
                    nc.tensor.matmul(o, ones[0:1, :], b_out_row[:, :], start=False, stop=True).then_inc(mixed[p], 1)

            def extend_row(p, b, s):
                if p == 0:
                    pe.wait_ge(mixed_read[0], b + 1)
                else:
                    pe.wait_ge(normed[p], b + 1)
                if not (isinstance(b, int) and b == 0):
                    pe.wait_ge(row_copied[p], b)
                pe.sem_inc(pe_go, 1)
                nc.tensor.transpose(bank_h[0:D, 0:P], row[:, s, 0:D], ident[:, :]).then_inc(row_in_pe[p], 1)
                pe.wait_ge(row_copied[p], b + 1)
                if not (isinstance(b, int) and b == 0):
                    if p == 0:
                        pe.wait_ge(row_ready[0], b)
                    else:
                        pe.wait_ge(own_ready[1], 2 * b)
                if p == 0:
                    nc.tensor.matmul(bank_a[:, 0:2 * H], row_turned[0:D, :], w_coef[1][:, :], start=True, stop=True)\
                        .then_inc(extra_made[p], 1)
                else:
                    nc.tensor.matmul(bank_a[:, 0:2 * D], row_turned[:, :], w_edge[:, :], start=True, stop=True)\
                        .then_inc(extra_made[p], 1)

            def heavy_blocks(p):
                for s in range(2):
                    pe.wait_ge(row_out[p][s], 16 * (NB // 2))
                pe.wait_ge(rounds_ready, 1)
                with pe.If(pe.value_load(most_rounds[0:1, 0:1], min_val=0, max_val=E) > 0):
                    done = pe.alloc_register(f"pe_done{p}")
                    pe.reg_mov(done, 0)
                    with pe.Fori(0, NB) as b:
                        with pe.If(pe.value_load(rounds[0:1, bass.ds(b, 1)], min_val=0, max_val=E) > 0):
                            h = pe.snap(done, min_val=0, max_val=NB)
                            turn_sums(p, h + NB, 0)
                            mix(p, h + NB, 0)
                            if p < 2:
                                extend_row(p, h + NB, 0)
                            pe.wait_ge(heavy_out[p], 16 * h + 16)
                            pe.reg_add(done, done, 1)

            for p in range(3):
                for run in RUNS:
                    with pairs_of(pe, run) as u:
                        for s in range(2):
                            b = 2 * u + s
                            if run[0] > 0 or s == 1:
                                mix(p, b - 1, 1 - s)
                                if p == 0:
                                    extend_row(p, b - 1, 1 - s)
                            if p == 1 and run[0] > 0:
                                extend_row(p, b - 2, s)
                            turn_sums(p, b, s)
                mix(p, NB - 1, 1)
                if p == 0:
                    extend_row(p, NB - 1, 1)
                if p == 1:
                    extend_row(p, NB - 2, 0)
                    extend_row(p, NB - 1, 1)
                heavy_blocks(p)


_INS = ['x', 'src', 'dst', 'L0_gnn_W1', 'L0_gnn_att_src1', 'L0_gnn_att_dst1', 'L0_gnn_b1', 'L0_gnn_lW1', 'L0_gnn_lb1',
        'L0_gnn_W2', 'L0_gnn_att_src2', 'L0_gnn_att_dst2', 'L0_gnn_b2', 'L0_gnn_lW2', 'L0_gnn_lb2',
        'L1_gnn_W_lin', 'L1_gnn_b_lin', 'L1_gnn_W_out', 'L1_gnn_b_out']


def kernel(**inputs):
    import numpy as np
    import concourse.bacc as bacc
    from concourse.bass_utils import run_bass_kernel_spmd

    nc = bacc.Bacc("TRN2", target_bir_lowering=False, num_devices=1)
    arrays, args = {}, []
    for name in _INS:
        a = np.ascontiguousarray(inputs[name])
        arrays[f"in_{name}"] = a
        args.append(nc.dram_tensor(f"in_{name}", a.shape, mybir.dt.from_np(a.dtype), kind="ExternalInput").ap())
    shape = inputs['x'].shape
    args.append(nc.dram_tensor("out_0", shape, F32, kind="ExternalOutput").ap())
    build(nc, *args)
    r = run_bass_kernel_spmd(nc, [arrays], core_ids=[0])
    return r.results[0]["out_0"]
```

```python
import math
from contextlib import ExitStack, contextmanager

import concourse.bass as bass
from concourse import mybir

F32 = mybir.dt.float32
I32 = mybir.dt.int32
ALU = mybir.AluOpType
ACT = mybir.ActivationFunctionType
AX = mybir.AxisListType

P = 128


def slots_per_block(n_nodes, n_edges, n_blocks):
    mean = n_edges / n_nodes
    share = [math.exp(k * math.log(mean) - mean - math.lgamma(k + 1)) for k in range(int(8 * mean) + 64)]

    def largest(rank, spread):
        k = 0
        while True:
            above = n_nodes * sum(share[k + 1:])
            if above + spread * math.sqrt(above) <= rank:
                return max(k, 2)
            k += 1

    return [largest(max(P * b, 2e-2), 3.0 if b else 0.0) for b in range(n_blocks)]


def runs_of_pairs(slots):
    runs, before = [], [0, 0]
    for u in range(len(slots) // 2):
        pair = slots[2 * u], slots[2 * u + 1]
        if u > 2 and runs[-1][2] == pair:
            runs[-1][1] += 1
        else:
            runs.append([u, 1, pair, tuple(before)])
        before = [before[0] + pair[0], before[1] + pair[1]]
    return runs


def landed_before(run, s, u):
    first, _, slots, before = run
    if s == 1:
        return landed(run, 0, u)
    return 16 * (slots[1] * (u - first) + before[1])


@contextmanager
def pairs_of(eng, run):
    first, count = run[0], run[1]
    if count == 1:
        yield first
    else:
        with eng.Fori(first, first + count) as u:
            yield u


def landed(run, s, u):
    first, _, slots, before = run
    return 16 * (slots[s] * (u - first) + before[s] + slots[s])


def build(nc, x, src, dst, W1, att_src1, att_dst1, b1, lW1, lb1, W2, att_src2, att_dst2, b2, lW2, lb2,
          W_lin, b_lin, W_out, b_out, out):
    N, D = x.shape
    E = src.shape[0]
    H = att_src1.shape[0]
    NB = -(-N // P)
    NP = NB * P
    assert NB % 14 == 0 and D == 64 and H == 4
    SLOTS = slots_per_block(N, E, NB)
    KMAX = SLOTS[0]
    RUNS = runs_of_pairs(SLOTS)
    assert RUNS[0][1] == RUNS[1][1] == 1
    COLS, COLS_V = 9, 4
    GROUPS = -(-(NB + 1) // COLS)
    SEG = min(k for k in range(1, E) if E % k == 0 and k >= COLS * E / N + 4 * math.sqrt(COLS * E / N))
    NSEG, WINDOW = E // SEG, 2 * SEG
    BELOW_MAX = NSEG - 2
    LOW_CLS = min(SLOTS[-1], SLOTS[1])
    CLS = SLOTS[1] + 2 - LOW_CLS
    PARTS = [(GROUPS * k // 3, GROUPS * (k + 1) // 3) for k in range(3)]
    TW = D + 2 * H
    PLACE, NODE, START, DEGREE = range(TW, TW + 4)
    TX = TW + 4
    LW = 2 * D
    OW = TX + TW
    OWN = (0, TX, 0)
    NEG, LOW = -1e30, -1e29
    ALPHA_EPS, LN_EPS, SLOPE = 1e-16, 1e-5, 0.2
    DEN_MIN = 1e-30
    FULL, REST = N // NB, N % NB

    ctx = ExitStack()
    with ctx:
        def sb(name, shape, dt=F32):
            return ctx.enter_context(nc.sbuf_tensor(name, shape, dt))

        def ps(name, shape):
            return ctx.enter_context(nc.psum_tensor(name, shape, F32))

        def sem(name):
            return ctx.enter_context(nc.semaphore(name))

        def scratch(name, shape, dt=F32):
            return nc.dram_tensor(name, shape, dt).ap()

        table1 = scratch("table1", [NP, TX])
        ordered = scratch("ordered", [NP, TX])
        place_of = scratch("place_of", [NP, 1], I32)
        table2 = scratch("table2", [NP, TW])
        table3 = scratch("table3", [NP, LW])
        src_padded = scratch("src_padded", [E + KMAX], I32)
        src_from = src_padded.rearrange("(a e) -> a e", a=1)

        half = 2 * KMAX * LW
        work = sb("work", [P, max(2 * half, NB * TX + 2 * CLS * NB + 14 * TX)])
        own = sb("own", [P, NB + 2, OW])
        idx_all = sb("idx_all", [P, NB + 1, KMAX], I32)
        rows_1 = work[:, 0:2 * KMAX * TX].rearrange("p (s k c) -> p s k c", s=2, k=KMAX)
        rows_2 = work[:, 0:2 * KMAX * TW].rearrange("p (s k c) -> p s k c", s=2, k=KMAX)
        rows_last = work[:, 0:half].rearrange("p (s k c) -> p s k c", s=2, k=KMAX)
        rows_of = (rows_1, rows_2, rows_last)
        weighted = work[:, half:2 * half]
        x_tab = work[:, 0:NB * TX].rearrange("p (b c) -> p b c", b=NB)
        at = NB * TX
        onehot = work[:, at:at + CLS * NB].rearrange("p (c b) -> p c b", c=CLS)
        onehot_flat = work[:, at:at + CLS * NB]
        prefix = work[:, at + CLS * NB:at + 2 * CLS * NB].rearrange("p (c b) -> p c b", c=CLS)
        prefix_flat = work[:, at + CLS * NB:at + 2 * CLS * NB]
        at += 2 * CLS * NB
        stage_e = work[:, at:at + 14 * TX].rearrange("p (j c) -> p j c", j=14)
        own_flat = own[:, :, :].rearrange("p b c -> p (b c)")
        windows = own_flat[:, 0:GROUPS * WINDOW].bitcast(I32).rearrange("p (g e) -> p g e", g=GROUPS)
        below = own_flat[:, GROUPS * WINDOW:(GROUPS + COLS) * WINDOW].rearrange("p (c e) -> p c e", c=COLS)
        below_flat = own_flat[:, GROUPS * WINDOW:(GROUPS + COLS) * WINDOW]
        assert (GROUPS + COLS) * WINDOW <= NB * OW and NSEG <= min(1024, COLS * WINDOW)

        ident = sb("ident", [P, P])
        before = sb("before", [P, P])
        after = sb("after", [P, P])
        ones = sb("ones", [P, P])
        slot_i = sb("slot_i", [P, KMAX], I32)
        slot_no = sb("slot_no", [P, KMAX])
        class_i = sb("class_i", [P, CLS], I32)
        class_no = sb("class_no", [P, CLS])
        node_i = sb("node_i", [P, COLS * GROUPS], I32)
        node_no = sb("node_no", [P, COLS * GROUPS])
        node_half = sb("node_half", [P, COLS * GROUPS])
        eps = sb("eps", [P, 1])
        zeros_i = sb("zeros_i", [1, KMAX], I32)
        last_i = sb("last_i", [1, NSEG], I32)
        last_f = sb("last_f", [1, NSEG])
        last_of_seg = sb("last_of_seg", [P, NSEG])
        segs_below = sb("segs_below", [P, GROUPS])
        window_at = sb("window_at", [P, GROUPS])
        window_at_i = sb("window_at_i", [P, GROUPS], I32)
        window_open = sb("window_open", [P, GROUPS])
        in_window = sb("in_window", [P, COLS * GROUPS])
        sign_sum = sb("sign_sum", [P, (COLS - COLS_V) * GROUPS])
        most_in = sb("most_in", [P, GROUPS])
        past_end = sb("past_end", [P, 1])
        again = sb("again", [1, 1], I32)
        again_at = sb("again_at", [P, 1])
        again_at_i = sb("again_at_i", [P, 1], I32)
        start = sb("start", [P, COLS * GROUPS])
        degree = sb("degree", [P, NB])
        capped = sb("capped", [P, NB])
        upto = sb("upto", [P, CLS + 1])
        place = sb("place", [P, NB])
        place_i = sb("place_i", [P, NB], I32)
        place_lo = sb("place_lo", [P, NB], I32)
        place_hi = sb("place_hi", [P, NB], I32)
        order_at = sb("order_at", [P, NB], I32)
        deg = sb("deg", [P, NB])
        has_edge = sb("has_edge", [P, NB])
        start_of = sb("start_of", [P, NB])
        node_of = sb("node_of", [P, NB], I32)
        order_now = sb("order_now", [P, 14], I32)
        start_now = sb("start_now", [P, 2], I32)
        most_col = sb("most_col", [NB, 1])
        slots_row = sb("slots_row", [1, NB])
        most_row = sb("most_row", [1, NB])
        rounds_row = sb("rounds_row", [1, NB])
        rounds = sb("rounds", [1, NB], I32)
        most_rounds = sb("most_rounds", [1, 1], I32)
        heavy_at = sb("heavy_at", [P, 1])
        heavy_at_i = sb("heavy_at_i", [P, 1], I32)
        heavy_left = sb("heavy_left", [P, 1])
        heavy_top = sb("heavy_top", [P, D])
        heavy_den = sb("heavy_den", [P, D])
        heavy_part = sb("heavy_part", [P, D])
        w_in = [sb(f"w_in{l}", [D, H * D]) for l in (1, 2)]
        att_in = [[sb(f"att_in{l}{k}", [D, H * D]) for k in "sd"] for l in (1, 2)]
        att_prod = sb("att_prod", [D, H * D])
        w_coef = [sb(f"w_coef{l}", [D, 2 * H]) for l in (1, 2)]
        w_heads = [sb(f"w_heads{l}", [P, 2, D]) for l in (1, 2)]
        w_self = [sb(f"w_self{l}", [D + 1, D]) for l in (1, 2)]
        bias_b = sb("bias_b", [D + 1, 2, D])
        w_lin_in = sb("w_lin_in", [D, 2 * D])
        w_edge = sb("w_edge", [D + 1, 2 * D])
        w_out_in = sb("w_out_in", [D, 2 * D])
        w_out = sb("w_out", [2 * D, D])
        b_out_row = sb("b_out_row", [1, D])
        x7 = sb("x7", [P, 7, D])
        xT7 = sb("xT7", [D, 7 * P])
        own_now = sb("own_now", [P, 2, D])
        idx_now = sb("idx_now", [P, 2, KMAX], I32)
        node_now = sb("node_now", [P, 2], I32)
        idle = sb("idle", [P, KMAX])
        logit = sb("logit", [P, KMAX + 1, H])
        heavy_prob = sb("heavy_prob", [P, KMAX + 1, H])
        top = sb("top", [P, H])
        psum_ = sb("psum_", [P, H])
        scale = sb("scale", [P, H])
        sums = sb("sums", [P, 2, H * D])
        turned = sb("turned", [P, 2 * P])
        own_turned = sb("own_turned", [D + 1, P])
        row_turned = sb("row_turned", [D + 1, P])
        row = sb("row", [P, 2, LW])
        pre = sb("pre", [P, 2, D])
        stat = sb("stat", [P, 6])
        mean_var = sb("mean_var", [P, 2, 2])
        std = sb("std", [P, 2])
        inv_std = sb("inv_std", [P, 1])
        den_c = sb("den_c", [P, D])
        den_more = sb("den_more", [P, D])
        num_c = sb("num_c", [P, D])

        bank_v = ps("bank_v", [P, 512])
        bank_o = [ps("bank_o0", [P, 512]), ps("bank_o1", [P, 512])]
        bank_h = ps("bank_h", [P, 512])
        bank_a = ps("bank_a", [P, 512])
        bank_t = ps("bank_t", [P, 1024])
        bank_s = ps("bank_s", [P, 512])
        assert KMAX * H <= 512 and 2 * D + KMAX <= 512
        prob = bank_s[:, 0:KMAX * H].rearrange("p (k h) -> p k h", h=H)
        target_c, top_c, idle_c = bank_s[:, 0:D], bank_s[:, D:2 * D], bank_s[:, 2 * D:2 * D + KMAX]
        KP = 1024 // D
        prob_c = bank_t[:, 0:KP * D].rearrange("p (k c) -> p k c", c=D)

        pool_go, dve_go, pe_go, sp_go = sem("pool_go"), sem("dve_go"), sem("pe_go"), sem("sp_go")
        consts_ready = sem("consts_ready")
        pool_zeroed = sem("pool_zeroed")
        x_zeroed = sem("x_zeroed")
        x_in = sem("x_in")
        last_in = sem("last_in")
        src_copied = sem("src_copied")
        weights_in = sem("weights_in")
        last_cast = sem("last_cast")
        last_spread = sem("last_spread")
        cleared = sem("cleared")
        prep_step = sem("prep_step")
        weights_ready = sem("weights_ready")
        lin_turned = sem("lin_turned")
        x_staged = sem("x_staged")
        x_turned = sem("x_turned")
        x_turned_copied = sem("x_turned_copied")
        coef_made = sem("coef_made")
        coef_stored = sem("coef_stored")
        table1_out = sem("table1_out")
        segs_counted = sem("segs_counted")
        window_staged = sem("window_staged")
        window_in = [sem(f"window_in{k}") for k in range(3)]
        counted_v = sem("counted_v")
        counted_a = sem("counted_a")
        past_end_found = sem("past_end_found")
        past_end_summed = sem("past_end_summed")
        again_ready = sem("again_ready")
        again_step = sem("again_step")
        again_staged = sem("again_staged")
        again_in = sem("again_in")
        counts_ready = sem("counts_ready")
        counts_summed = sem("counts_summed")
        places_ready = sem("places_ready")
        entry_staged = [sem(f"entry_staged{k}") for k in range(2)]
        entry_out = [sem(f"entry_out{k}") for k in range(2)]
        place_out = sem("place_out")
        own_in = [sem(f"own_in{k}") for k in range(2)]
        own_padded = sem("own_padded")
        idx_zeroed = sem("idx_zeroed")
        degs_ready = sem("degs_ready")
        degs_turned = sem("degs_turned")
        most_found = sem("most_found")
        most_turned = sem("most_turned")
        rounds_step = sem("rounds_step")
        rounds_ready = sem("rounds_ready")

        def per_pass(name, passes=(0, 1, 2)):
            return {p: sem(f"{name}_{p}") for p in passes}

        def per_pass_and_parity(name, passes=(0, 1, 2)):
            return {p: [sem(f"{name}_{p}{s}") for s in range(2)] for p in passes}

        idx_ready = per_pass_and_parity("idx_ready", (1, 2))
        start_staged = [sem(f"start_staged{s}") for s in range(2)]
        idx_in = [sem(f"idx_in{s}") for s in range(2)]
        places_kept = [sem(f"places_kept{s}") for s in range(2)]
        rows_in = per_pass_and_parity("rows_in")
        rows_used = per_pass_and_parity("rows_used")
        front_step = per_pass("front_step")
        logits_ready = per_pass("logits_ready")
        probs_ready = per_pass("probs_ready")
        sum_step = per_pass("sum_step")
        sums_ready = per_pass("sums_ready")
        own_staged = per_pass("own_staged", (0, 1))
        sums_turned = per_pass("sums_turned")
        turned_copied = per_pass("turned_copied")
        mixed = per_pass("mixed")
        mixed_read = per_pass("mixed_read")
        stat_step = per_pass("stat_step", (1, 2))
        stats_ready = per_pass("stats_ready", (1, 2))
        std_ready = per_pass("std_ready", (1, 2))
        norm_step = per_pass("norm_step", (1, 2))
        normed = per_pass("normed", (1, 2))
        row_in_pe = per_pass("row_in_pe", (0, 1))
        row_copied = per_pass("row_copied", (0, 1))
        extra_made = per_pass("extra_made", (0, 1))
        row_ready = per_pass("row_ready")
        own_ready = per_pass("own_ready", (0, 1))
        row_out = per_pass_and_parity("row_out")
        heavy_own = sem("heavy_own")
        heavy_init = per_pass("heavy_init")
        heavy_staged = sem("heavy_staged")
        heavy_idx = sem("heavy_idx")
        heavy_place = sem("heavy_place")
        heavy_rows = sem("heavy_rows")
        heavy_arrived = sem("heavy_arrived")
        heavy_step = sem("heavy_step")
        heavy_logits = sem("heavy_logits")
        heavy_probs = sem("heavy_probs")
        heavy_sum = sem("heavy_sum")
        heavy_end = per_pass("heavy_end")
        heavy_out = per_pass("heavy_out")

        N_WEIGHT_LOADS = 2 * (1 + 2 + H + 3) + 4

        def one(ap):
            return ap.rearrange("p a c -> p (a c)")

        ctx.enter_context(nc.allow_non_contiguous_dma(reason="the last edge of each segment"))
        block = ctx.enter_context(nc.Block())

        @block.sync
        def _(sp):
            sp.dma_start(last_i[:, :], dst.rearrange("(s e) -> s e", e=SEG)[:, SEG - 1:SEG]
                         .rearrange("s e -> e s")).then_inc(last_in, 16)
            layers = ((W1, att_src1, att_dst1, b1, lW1, lb1), (W2, att_src2, att_dst2, b2, lW2, lb2))
            for l, (W, a_s, a_d, b, lW, lb) in enumerate(layers):
                sp.dma_start(w_in[l][:, :], W).then_inc(weights_in, 16)
                for k, a in enumerate((a_s, a_d)):
                    sp.dma_start(att_in[l][k][:, :], a.rearrange("h c -> (h c)").partition_broadcast(D))\
                        .then_inc(weights_in, 16)
                for h in range(H):
                    sp.dma_start(w_heads[l][D * (h % 2):D * (h % 2) + D, h // 2, :], W[:, D * h:D * h + D])\
                        .then_inc(weights_in, 16)
                sp.dma_start(w_self[l][0:D, :], lW).then_inc(weights_in, 16)
                sp.dma_start(bias_b[D:D + 1, l, :], b.rearrange("(a c) -> a c", a=1)).then_inc(weights_in, 16)
                sp.dma_start(w_self[l][D:D + 1, :], lb.rearrange("(a c) -> a c", a=1)).then_inc(weights_in, 16)
            sp.dma_start(w_lin_in[:, :], W_lin[0:D, :]).then_inc(weights_in, 16)
            sp.dma_start(w_edge[D:D + 1, D:2 * D], b_lin[0:D].rearrange("(a c) -> a c", a=1))\
                .then_inc(weights_in, 16)
            sp.dma_start(w_out_in[:, :], W_out).then_inc(weights_in, 16)
            sp.dma_start(b_out_row[:, :], b_out.rearrange("(a c) -> a c", a=1)).then_inc(weights_in, 16)
            sp.wait_ge(window_in[2], 16 * (PARTS[2][1] - PARTS[2][0]))
            sp.wait_ge(x_zeroed, 1)
            sp.dma_start(x_tab[0:FULL, :, 0:D], x[0:FULL * NB, :].rearrange("(p b) c -> p b c", b=NB))\
                .then_inc(x_in, 16)
            sp.dma_start(x_tab[FULL:FULL + 1, 0:REST, 0:D],
                         x[FULL * NB:N, :].rearrange("(p b) c -> p b c", p=1)).then_inc(x_in, 16)
            sp.wait_ge(pool_zeroed, 1)
            sp.dma_start(src_padded[0:E].rearrange("(q e) -> q e", e=SEG),
                         src.rearrange("(q e) -> q e", e=SEG)).then_inc(src_copied, 16)
            sp.dma_start(src_padded[E:E + KMAX].rearrange("(a e) -> a e", a=1), zeros_i[:, :])\
                .then_inc(src_copied, 16)
            sp.wait_ge(coef_stored, NB // 7)
            sp.wait_ge(places_ready, 5)
            sp.dma_start(table1.rearrange("(p b) c -> p b c", b=NB), x_tab).then_inc(table1_out, 16)
            sp.dma_start(place_of.rearrange("(p b) a -> p (b a)", b=NB), place_i[:, :]).then_inc(place_out, 16)
            for k in range(2):
                sp.wait_ge(entry_out[k], 16 * 7 * (NB // 14))
            by_place = ordered.rearrange("(p b) c -> p b c", b=NB)
            sp.dma_start(own[:, 0:14, 0:TX], by_place[:, 0:14, :]).then_inc(own_in[0], 16)
            sp.wait_ge(idx_in[0], 16)
            for b0 in range(14, NB, 14):
                sp.dma_start(own[:, b0:b0 + 14, 0:TX], by_place[:, b0:b0 + 14, :]).then_inc(own_in[1], 16)

            for p, (table, width) in enumerate(((table2, TW), (table3, LW))):
                with sp.Fori(0, NB // 2) as u:
                    for s in range(2):
                        sp.wait_ge(row_ready[p], 2 * u + s + 1)
                        sp.sem_inc(sp_go, 1)
                        sp.dma_start(table[bass.ds((2 * u + s) * P, P), :], row[:, s, 0:width])\
                            .then_inc(row_out[p][s], 16)
                for s in range(2):
                    sp.wait_ge(row_out[p][s], 16 * (NB // 2))
                sp.wait_ge(rounds_ready, 1)
                with sp.If(sp.value_load(most_rounds[0:1, 0:1], min_val=0, max_val=E) > 0):
                    done = sp.alloc_register(f"sp_done{p}")
                    sp.reg_mov(done, 0)
                    with sp.Fori(0, NB) as b:
                        with sp.If(sp.value_load(rounds[0:1, bass.ds(b, 1)], min_val=0, max_val=E) > 0):
                            h = sp.snap(done, min_val=0, max_val=NB)
                            sp.wait_ge(row_ready[p], h + NB + 1)
                            sp.sem_inc(sp_go, 1)
                            sp.dma_start(table[bass.ds(b * P, P), :], row[:, 0, 0:width]).then_inc(heavy_out[p], 16)
                            sp.wait_ge(heavy_out[p], 16 * h + 16)
                            sp.sem_inc(sp_go, 1)
                            sp.reg_add(done, done, 1)

        @block.gpsimd
        def _(pool):
            nc.gpsimd.memset(zeros_i[:, :], 0).then_inc(pool_zeroed, 1)
            nc.gpsimd.iota(node_i[:, :], [[1, COLS * GROUPS]], base=0, channel_multiplier=NB).then_inc(consts_ready, 1)
            nc.gpsimd.memset(ident[:, :], 0.0).then_inc(consts_ready, 1)
            nc.gpsimd.memset(before[:, :], 1.0).then_inc(consts_ready, 1)
            nc.gpsimd.memset(after[:, :], 1.0).then_inc(consts_ready, 1)
            nc.gpsimd.memset(ones[:, :], 1.0).then_inc(consts_ready, 1)
            nc.gpsimd.iota(slot_i[:, :], [[1, KMAX]], base=0, channel_multiplier=0).then_inc(consts_ready, 1)
            nc.gpsimd.iota(class_i[:, :], [[-1, CLS]], base=LOW_CLS + CLS - 1, channel_multiplier=0).then_inc(consts_ready, 1)
            pool.wait_ge(consts_ready, 7)
            nc.gpsimd.affine_select(out=ident[:, :], in_=ident[:, :], compare_op=ALU.not_equal, fill=1.0,
                                    base=0, pattern=[[-1, P]], channel_multiplier=1).then_inc(consts_ready, 1)
            nc.gpsimd.affine_select(out=before[:, :], in_=before[:, :], compare_op=ALU.is_gt, fill=0.0,
                                    base=0, pattern=[[1, P]], channel_multiplier=-1).then_inc(consts_ready, 1)
            nc.gpsimd.affine_select(out=after[:, :], in_=after[:, :], compare_op=ALU.is_gt, fill=0.0,
                                    base=0, pattern=[[-1, P]], channel_multiplier=1).then_inc(consts_ready, 1)

            pool.wait_ge(consts_ready, 10)
            nc.gpsimd.memset(x_tab[96:P, REST:NB, :], 0.0).then_inc(x_zeroed, 1)

            def fetch_window(to, at):
                return nc.gpsimd.indirect_dma_start(to, None, dst.rearrange("(a e) -> a e", a=1),
                                                    bass.IndirectOffsetOnAxis(ap=at, axis=1))

            for k, (g0, g1) in enumerate(PARTS):
                pool.wait_ge(window_staged, k + 1)
                for g in range(g0, g1):
                    fetch_window(windows[:, g, :], window_at_i[:, g:g + 1]).then_inc(window_in[k], 16)
            pool.wait_ge(again_ready, 1)
            with pool.If(pool.value_load(again[0:1, 0:1], min_val=0, max_val=P * GROUPS) > 0):
                with pool.Fori(0, NB + 1) as n:
                    pool.wait_ge(again_staged, n + 1)
                    pool.sem_inc(pool_go, 1)
                    fetch_window(windows[:, 0, :], again_at_i[:, 0:1]).then_inc(again_in, 16)

            with pool.Fori(0, NB // 14) as j:
                for k in range(2):
                    pool.wait_ge(entry_staged[k], 2 * j + 2)
                    pool.sem_inc(pool_go, 1)
                    for c in range(7 * k, 7 * k + 7):
                        nc.gpsimd.indirect_dma_start(
                            ordered, bass.IndirectOffsetOnAxis(ap=order_now[:, c:c + 1], axis=0),
                            stage_e[:, c, :], None).then_inc(entry_out[k], 16)

            def gather(p, table, s, k):
                nc.gpsimd.indirect_dma_start(rows_of[p][:, s, k, :], None, table,
                                             bass.IndirectOffsetOnAxis(ap=idx_now[:, s, k:k + 1], axis=0))\
                    .then_inc(rows_in[p][s], 16)

            def fetch_sources(s):
                nc.gpsimd.indirect_dma_start(idx_now[:, s, :], None, src_from,
                                             bass.IndirectOffsetOnAxis(ap=start_now[:, s:s + 1], axis=1))\
                    .then_inc(idx_in[s], 16)

            def scatter(n, s, written):
                pool.wait_ge(row_ready[2], n + 1)
                pool.sem_inc(pool_go, 1)
                nc.gpsimd.indirect_dma_start(out, bass.IndirectOffsetOnAxis(ap=node_now[:, s:s + 1], axis=0),
                                             row[:, s, 0:D], None, bounds_check=N - 1, oob_is_err=False)\
                    .then_inc(written, 16)

            turn = pool.alloc_register("pool_turn")
            pool.reg_mov(turn, 0)

            def take_back(semaphore, count):
                nc.gpsimd.inc_swdge_sem([semaphore], [count], mode="sub")

            def heavy_gathers(p, table):
                with pool.If(pool.value_load(most_rounds[0:1, 0:1], min_val=0, max_val=E) > 0):
                    done = pool.alloc_register(f"pool_done{p}")
                    pool.reg_mov(done, 0)
                    with pool.Fori(0, NB) as b:
                        n_rounds = pool.value_load(rounds[0:1, bass.ds(b, 1)], min_val=0, max_val=E)
                        with pool.If(n_rounds > 0):
                            h = pool.snap(done, min_val=0, max_val=NB)
                            if p == 1:
                                first = nc.gpsimd.dma_start(
                                    own[:, bass.ds(b, 1), 0:TX],
                                    ordered.rearrange("(p b) c -> p b c", b=NB)[:, bass.ds(b, 1), :])
                                first.then_inc(heavy_own, 16)
                                nc.gpsimd.dma_start(own[:, bass.ds(b, 1), TX:OW].rearrange("p a c -> p (a c)"),
                                                    table2[bass.ds(b * P, P), :]).then_inc(heavy_own, 16)
                            with pool.Fori(0, n_rounds) as r:
                                g = pool.snap(turn, min_val=0, max_val=3 * E)
                                pool.wait_ge(heavy_staged, g + 1)
                                pool.sem_inc(pool_go, 1)
                                nc.gpsimd.indirect_dma_start(
                                    idx_now[:, 0, :], None, src_from,
                                    bass.IndirectOffsetOnAxis(ap=heavy_at_i[:, 0:1], axis=1)).then_inc(heavy_idx, 16)
                                pool.wait_ge(heavy_idx, 16)
                                take_back(heavy_idx, 16)
                                if p > 0:
                                    for k in range(KMAX):
                                        nc.gpsimd.indirect_dma_start(
                                            idx_now[:, 1, k:k + 1], None, place_of,
                                            bass.IndirectOffsetOnAxis(ap=idx_now[:, 0, k:k + 1], axis=0))\
                                            .then_inc(heavy_place, 16)
                                    pool.wait_ge(heavy_place, 16 * KMAX)
                                    take_back(heavy_place, 16 * KMAX)
                                for k in range(KMAX):
                                    nc.gpsimd.indirect_dma_start(
                                        rows_of[p][:, 0, k, :], None, table,
                                        bass.IndirectOffsetOnAxis(ap=idx_now[:, min(p, 1), k:k + 1], axis=0))\
                                        .then_inc(heavy_rows, 16)
                                pool.wait_ge(heavy_rows, 16 * KMAX)
                                take_back(heavy_rows, 16 * KMAX)
                                pool.sem_inc(heavy_arrived, 1)
                                pool.reg_add(turn, turn, 1)
                            if p == 2:
                                scatter(h + NB, 0, heavy_out[2])
                            pool.wait_ge(heavy_out[p], 16 * h + 16)
                            pool.reg_add(done, done, 1)

            for p, table in enumerate((table1, table2, table3)):
                if p == 0:
                    pool.wait_ge(src_copied, 32)
                    pool.wait_ge(table1_out, 16)
                    pool.wait_ge(start_staged[0], 1)
                    fetch_sources(0)
                else:
                    for s in range(2):
                        pool.wait_ge(row_out[p - 1][s], 16 * (NB // 2))
                        pool.wait_ge(rows_used[p - 1][s], NB // 2)
                for run in RUNS:
                    with pairs_of(pool, run) as u:
                        for s in range(2):
                            b, K = 2 * u + s, run[2][s]
                            if p == 0:
                                pool.wait_ge(idx_in[s], 16 * u + 16)
                            else:
                                pool.wait_ge(idx_ready[p][s], u + 1)
                            if run[0] > 0:
                                pool.wait_ge(rows_used[p][s], u)
                                if p == 0:
                                    pool.wait_ge(places_kept[s], u)
                            pool.sem_inc(pool_go, 1)
                            for k in range(K // 2 if p == 0 else K):
                                gather(p, table, s, k)
                            if p == 0:
                                pool.wait_ge(start_staged[1 - s], u + s + 1)
                                if run[0] > 0 or s == 1:
                                    pool.wait_ge(rows_in[0][1 - s], landed_before(run, s, u))
                                pool.sem_inc(pool_go, 1)
                                fetch_sources(1 - s)
                                for k in range(K // 2, K):
                                    gather(p, table, s, k)
                            if p == 2 and (run[0] > 1 or (run[0] == 1 and s == 1)):
                                scatter(b - 3, 1 - s, row_out[2][1 - s])
                if p == 2:
                    for b in range(NB - 3, NB):
                        scatter(b, b % 2, row_out[2][b % 2])
                for s in range(2):
                    pool.wait_ge(row_out[p][s], 16 * (NB // 2))
                if p == 0:
                    pool.wait_ge(place_out, 16)
                    pool.wait_ge(idx_in[0], 16 * (NB // 2) + 16)
                    pool.wait_ge(rounds_ready, 1)
                heavy_gathers(p, table)

        @block.vector
        def _(dve):
            dve.wait_ge(last_in, 16)
            nc.vector.tensor_copy(last_f[:, :], last_i[:, :]).then_inc(last_cast, 1)
            dve.wait_ge(consts_ready, 10)
            nc.vector.tensor_copy(node_no[:, :], node_i[:, :]).then_inc(prep_step, 1)
            nc.vector.tensor_copy(slot_no[:, :], slot_i[:, :]).then_inc(prep_step, 1)
            nc.vector.tensor_copy(class_no[:, :], class_i[:, :]).then_inc(prep_step, 1)
            dve.wait_ge(last_spread, 1)
            nc.vector.tensor_copy(last_of_seg[:, :], bank_t[:, 0:NSEG]).then_inc(prep_step, 1)
            dve.wait_ge(prep_step, 4)
            nc.vector.tensor_scalar(node_half[:, :], node_no[:, :], -0.5, None, ALU.add).then_inc(prep_step, 1)
            dve.sem_inc(segs_counted, 1)
            dve.sem_inc(counted_v, COLS_V)
            for k, (g0, g1) in enumerate(PARTS):
                with dve.Fori(g0, g1) as g:
                    dve.wait_ge(segs_counted, g + 1)
                    nc.vector.tensor_scalar(below_flat[:, 0:BELOW_MAX], last_of_seg[:, 0:BELOW_MAX],
                                            node_no[:, bass.ds(COLS * g, 1)], None, ALU.is_lt, ALU.add,
                                            accum_out=segs_below[:, bass.ds(g, 1)]).then_inc(segs_counted, 1)
                dve.wait_ge(segs_counted, g1 + 1)
                nc.vector.tensor_scalar(window_at_i[:, g0:g1], segs_below[:, g0:g1], float(SEG), None, ALU.mult)\
                    .then_inc(window_staged, 1)
            nc.vector.tensor_scalar(window_at[:, :], segs_below[:, :], float(SEG), None, ALU.mult)\
                .then_inc(segs_counted, 1)
            nc.vector.tensor_scalar(window_open[:, :], segs_below[:, :], float(BELOW_MAX), None, ALU.is_lt)\
                .then_inc(segs_counted, 1)
            dve.wait_ge(weights_in, 16 * N_WEIGHT_LOADS)
            n_w = 0
            for l in range(2):
                for k in range(2):
                    if n_w:
                        dve.wait_ge(weights_ready, n_w)
                    nc.vector.tensor_tensor(att_prod[:, :], w_in[l][:, :], att_in[l][k][:, :], ALU.mult)\
                        .then_inc(weights_ready, 1)
                    dve.wait_ge(weights_ready, n_w + 1)
                    nc.vector.tensor_reduce(w_coef[l][:, H * k:H * k + H],
                                            att_prod[:, :].rearrange("p (h c) -> p h c", h=H), AX.X, ALU.add)\
                        .then_inc(weights_ready, 1)
                    n_w += 2
                nc.vector.tensor_tensor(w_self[l][D:D + 1, :], w_self[l][D:D + 1, :], bias_b[D:D + 1, l, :],
                                        ALU.add).then_inc(weights_ready, 1)
                n_w += 1
            dve.wait_ge(lin_turned, 1)
            nc.vector.tensor_copy(w_edge[0:D, :], bank_h[0:D, 0:2 * D]).then_inc(weights_ready, 1)
            nc.vector.tensor_copy(w_out[:, :], bank_h[:, 2 * D:3 * D]).then_inc(weights_ready, 1)

            dve.wait_ge(segs_counted, GROUPS + 3)
            for k, (g0, g1) in enumerate(PARTS):
                dve.wait_ge(window_in[k], 16 * (g1 - g0))
                dve.sem_inc(dve_go, 1)
                with dve.Fori(g0, g1) as g:
                    for c in range(COLS_V):
                        dve.wait_ge(counted_v, COLS_V * g + c + 1)
                        nc.vector.tensor_scalar(below[:, c, :], one(windows[:, bass.ds(g, 1), :]),
                                                node_no[:, bass.ds(COLS * g + c, 1)], None, ALU.is_lt, ALU.add,
                                                accum_out=in_window[:, bass.ds(COLS * g + c, 1)])\
                            .then_inc(counted_v, 1)
            dve.wait_ge(counted_a, (COLS - COLS_V) * (GROUPS + 1))
            by_group = in_window[:, :].rearrange("p (g c) -> p g c", c=COLS)
            nc.vector.tensor_scalar(by_group[:, :, COLS_V:COLS], sign_sum[:, :].rearrange("p (g c) -> p g c", g=GROUPS),
                                    0.5, 0.5 * WINDOW, ALU.mult, ALU.add).then_inc(counted_v, 1)
            dve.wait_ge(counted_v, COLS_V * (GROUPS + 1) + 1)
            nc.vector.tensor_reduce(most_in[:, :], by_group, AX.X, ALU.max).then_inc(counted_v, 1)
            s0 = 5
            nc.vector.tensor_tensor(start[:, :].rearrange("p (g c) -> p g c", c=COLS), by_group,
                                    window_at[:, :].unsqueeze(2).to_broadcast([P, GROUPS, COLS]), ALU.add)\
                .then_inc(prep_step, 1)
            dve.wait_ge(counted_v, COLS_V * (GROUPS + 1) + 2)
            nc.vector.scalar_tensor_tensor(out=most_in[:, :], in0=most_in[:, :], scalar=float(WINDOW),
                                           in1=window_open[:, :], op0=ALU.is_ge, op1=ALU.mult).then_inc(counted_v, 1)
            dve.wait_ge(counted_v, COLS_V * (GROUPS + 1) + 3)
            nc.vector.tensor_reduce(past_end[:, :], most_in[:, :], AX.X, ALU.add).then_inc(past_end_found, 1)
            dve.wait_ge(past_end_summed, 1)
            nc.vector.tensor_copy(again[:, :], bank_s[0:1, 0:1]).then_inc(again_ready, 1)
            dve.wait_ge(again_ready, 1)
            dve.wait_ge(prep_step, s0 + 1)
            with dve.If(dve.value_load(again[0:1, 0:1], min_val=0, max_val=P * GROUPS) > 0):
                with dve.Fori(0, NB + 1) as n:
                    nc.vector.tensor_scalar(below_flat[:, 0:BELOW_MAX], last_of_seg[:, 0:BELOW_MAX],
                                            node_no[:, bass.ds(n, 1)], None, ALU.is_lt, ALU.add,
                                            accum_out=past_end[:, :]).then_inc(again_step, 1)
                    dve.wait_ge(again_step, 4 * n + 1)
                    nc.vector.tensor_scalar(again_at[:, :], past_end[:, :], float(SEG), None, ALU.mult)\
                        .then_inc(again_step, 1)
                    nc.vector.tensor_scalar(again_at_i[:, :], past_end[:, :], float(SEG), None, ALU.mult)\
                        .then_inc(again_staged, 1)
                    dve.wait_ge(again_in, 16 * n + 16)
                    dve.wait_ge(again_step, 4 * n + 2)
                    nc.vector.tensor_scalar(below[:, 0, :], windows[:, 0, :], node_no[:, bass.ds(n, 1)], None,
                                            ALU.is_lt, ALU.add, accum_out=past_end[:, :]).then_inc(again_step, 1)
                    dve.wait_ge(again_step, 4 * n + 3)
                    nc.vector.tensor_tensor(start[:, bass.ds(n, 1)], past_end[:, :], again_at[:, :], ALU.add)\
                        .then_inc(again_step, 1)
                    dve.wait_ge(again_step, 4 * n + 4)
                    dve.sem_inc(dve_go, 1)

            dve.wait_ge(prep_step, s0 + 1)
            nc.vector.tensor_tensor(degree[:, :], start[:, 1:NB + 1], start[:, 0:NB], ALU.subtract)\
                .then_inc(prep_step, 1)
            dve.wait_ge(prep_step, s0 + 2)
            dve.wait_ge(x_zeroed, 1)
            nc.vector.tensor_copy(x_tab[:, :, NODE], node_no[:, 0:NB]).then_inc(places_ready, 1)
            nc.vector.tensor_copy(x_tab[:, :, START], start[:, 0:NB]).then_inc(places_ready, 1)
            nc.vector.tensor_copy(x_tab[:, :, DEGREE], degree[:, :]).then_inc(places_ready, 1)
            nc.vector.tensor_scalar(capped[:, :], degree[:, :], float(LOW_CLS), float(LOW_CLS + CLS - 1), ALU.max,
                                    ALU.min).then_inc(prep_step, 1)
            nc.vector.memset(upto[:, 0:1], 0.0).then_inc(counts_ready, 1)
            dve.wait_ge(prep_step, s0 + 3)
            nc.vector.tensor_tensor(onehot, capped[:, :].unsqueeze(1).to_broadcast([P, CLS, NB]),
                                    class_no[:, :].unsqueeze(2).to_broadcast([P, CLS, NB]), ALU.is_equal)\
                .then_inc(prep_step, 1)
            dve.wait_ge(prep_step, s0 + 4)
            nc.vector.tensor_tensor_scan(prefix_flat, onehot_flat, onehot_flat, 0.0, ALU.add, ALU.max)\
                .then_inc(prep_step, 1)
            dve.wait_ge(prep_step, s0 + 5)
            nc.vector.tensor_copy(upto[:, 1:CLS + 1], prefix[:, :, NB - 1]).then_inc(counts_ready, 1)
            dve.wait_ge(counts_summed, 1)
            nc.vector.scalar_tensor_tensor(out=prefix, in0=prefix, scalar=-1.0,
                                           in1=bank_s[:, 0:CLS].unsqueeze(2).to_broadcast([P, CLS, NB]),
                                           op0=ALU.add, op1=ALU.add).then_inc(prep_step, 1)
            dve.wait_ge(prep_step, s0 + 6)
            nc.vector.tensor_tensor(prefix, prefix, onehot, ALU.mult).then_inc(prep_step, 1)
            dve.wait_ge(prep_step, s0 + 7)
            nc.vector.tensor_reduce(place[:, :], prefix.rearrange("p c b -> p b c"), AX.X, ALU.add)\
                .then_inc(prep_step, 1)
            dve.wait_ge(prep_step, s0 + 8)
            nc.vector.tensor_copy(place_i[:, :], place[:, :]).then_inc(prep_step, 1)
            nc.vector.tensor_copy(x_tab[:, :, PLACE], place[:, :]).then_inc(places_ready, 1)
            dve.wait_ge(prep_step, s0 + 9)
            nc.vector.tensor_single_scalar(place_lo[:, :], place_i[:, :], P - 1, ALU.bitwise_and).then_inc(prep_step, 1)
            nc.vector.tensor_single_scalar(place_hi[:, :], place_i[:, :], P.bit_length() - 1,
                                           ALU.logical_shift_right).then_inc(prep_step, 1)
            dve.wait_ge(prep_step, s0 + 11)
            nc.vector.scalar_tensor_tensor(out=order_at[:, :], in0=place_lo[:, :], scalar=float(NB),
                                           in1=place_hi[:, :], op0=ALU.mult, op1=ALU.add).then_inc(places_ready, 1)

            nc.vector.memset(own[:, NB:NB + 2, :], 0.0).then_inc(own_padded, 1)
            nc.vector.memset(eps[:, :], LN_EPS).then_inc(cleared, 1)
            nc.vector.memset(idx_all[:, :, :], 0).then_inc(cleared, 1)
            nc.vector.memset(own_turned[D:D + 1, :], 1.0).then_inc(cleared, 1)
            nc.vector.memset(row_turned[D:D + 1, :], 1.0).then_inc(cleared, 1)
            nc.vector.memset(w_edge[D:D + 1, 0:D], 0.0).then_inc(cleared, 1)
            for first, pairs, slots, _ in RUNS:
                of_run = slots_row[0:1, 2 * first:2 * first + 2 * pairs].rearrange("a (u s) -> a u s", s=2)
                if slots[0] == slots[1]:
                    last = nc.vector.memset(of_run, float(slots[0]))
                else:
                    nc.vector.memset(of_run[:, :, 0], float(slots[0]))
                    last = nc.vector.memset(of_run[:, :, 1], float(slots[1]))
            last.then_inc(cleared, 1)
            dve.wait_ge(own_in[0], 16)
            dve.wait_ge(own_in[1], 16 * (NB // 14 - 1))
            nc.vector.tensor_copy(deg[:, :], own[:, 0:NB, DEGREE]).then_inc(degs_ready, 1)
            nc.vector.tensor_copy(start_of[:, :], own[:, 0:NB, START]).then_inc(degs_ready, 1)
            nc.vector.tensor_copy(node_of[:, :], own[:, 0:NB, NODE]).then_inc(degs_ready, 1)
            dve.wait_ge(degs_ready, 3)
            nc.vector.tensor_scalar(has_edge[:, :], deg[:, :], 1.0, None, ALU.min).then_inc(degs_ready, 1)
            dve.wait_ge(degs_turned, 1)
            nc.vector.tensor_reduce(most_col[:, :], bank_s[0:NB, 0:P], AX.X, ALU.max).then_inc(most_found, 1)
            dve.wait_ge(most_turned, 1)
            nc.vector.tensor_copy(most_row[:, :], bank_s[0:1, 0:NB]).then_inc(rounds_step, 1)
            dve.wait_ge(rounds_step, 1)
            nc.vector.tensor_tensor(slots_row[:, :], most_row[:, :], slots_row[:, :], ALU.is_gt)\
                .then_inc(rounds_step, 1)
            nc.vector.tensor_scalar(rounds_row[:, :], most_row[:, :], 1.0 / KMAX, 1.0, ALU.mult, ALU.add)\
                .then_inc(rounds_step, 1)
            dve.wait_ge(rounds_step, 3)
            nc.vector.tensor_tensor(rounds[:, :], rounds_row[:, :], slots_row[:, :], ALU.mult).then_inc(rounds_step, 1)
            dve.wait_ge(rounds_step, 4)
            nc.vector.tensor_reduce(most_rounds[:, :], rounds[:, :], AX.X, ALU.max).then_inc(rounds_ready, 1)
            dve.wait_ge(degs_ready, 4)

            def gat_front(p, b, s, K, arrived):
                n = 6 * b
                mine = own[:, bass.ds(b, 1), OWN[p] + D + H:OWN[p] + TW]
                lg, idl = logit[:, 0:K, :], idle[:, 0:K]
                dve.wait_ge(rows_in[p][s], arrived)
                nc.vector.tensor_tensor(lg, rows_of[p][:, s, 0:K, D:D + H], mine.to_broadcast([P, K, H]), ALU.add)\
                    .then_inc(front_step[p], 1)
                nc.vector.tensor_scalar(idl, slot_no[:, 0:K], deg[:, bass.ds(b, 1)], NEG, ALU.is_ge, ALU.mult)\
                    .then_inc(front_step[p], 1)
                dve.wait_ge(front_step[p], n + 1)
                nc.vector.scalar_tensor_tensor(out=lg, in0=lg, scalar=SLOPE, in1=lg, op0=ALU.mult, op1=ALU.max)\
                    .then_inc(front_step[p], 1)
                dve.wait_ge(front_step[p], n + 3)
                nc.vector.tensor_tensor(lg, lg, idl.unsqueeze(2).to_broadcast([P, K, H]), ALU.add)\
                    .then_inc(front_step[p], 1)
                dve.wait_ge(front_step[p], n + 4)
                nc.vector.tensor_reduce(top[:, :], lg.rearrange("p k h -> p h k"), AX.X, ALU.max)\
                    .then_inc(front_step[p], 1)
                dve.wait_ge(front_step[p], n + 5)
                nc.vector.tensor_scalar(top[:, :], top[:, :], LOW, None, ALU.max).then_inc(front_step[p], 1)
                dve.wait_ge(front_step[p], n + 6)
                nc.vector.tensor_tensor(lg, lg, top[:, :].unsqueeze(1).to_broadcast([P, K, H]), ALU.subtract)\
                    .then_inc(logits_ready[p], 1)

            def gat_sums(p, b, s, K):
                n = 5 * b
                pr = prob[:, 0:K, :]
                prod = weighted[:, 0:H * K * D].rearrange("p (h k c) -> p h k c", h=H, k=K)
                dve.wait_ge(probs_ready[p], b + 1)
                nc.vector.tensor_reduce(psum_[:, :], pr.rearrange("p k h -> p h k"), AX.X, ALU.add)\
                    .then_inc(sum_step[p], 1)
                dve.wait_ge(sum_step[p], n + 1)
                nc.vector.tensor_scalar(psum_[:, :], psum_[:, :], ALPHA_EPS, float(H), ALU.add, ALU.mult)\
                    .then_inc(sum_step[p], 1)
                dve.wait_ge(sum_step[p], n + 2)
                nc.vector.reciprocal(scale[:, :], psum_[:, :]).then_inc(sum_step[p], 1)
                dve.wait_ge(sum_step[p], n + 3)
                nc.vector.tensor_tensor(pr, pr, scale[:, :].unsqueeze(1).to_broadcast([P, K, H]), ALU.mult)\
                    .then_inc(sum_step[p], 1)
                dve.wait_ge(sum_step[p], n + 4)
                if not (isinstance(b, int) and b == 0):
                    dve.wait_ge(sums_ready[p], b)
                nc.vector.tensor_tensor(
                    prod, rows_of[p][:, s, 0:K, 0:D].unsqueeze(1).to_broadcast([P, H, K, D]),
                    pr.rearrange("p k h -> p h k").unsqueeze(3).to_broadcast([P, H, K, D]), ALU.mult)\
                    .then_inc(sum_step[p], 1)
                dve.wait_ge(sum_step[p], n + 5)
                dve.sem_inc(rows_used[p][s], 1)
                if not (isinstance(b, int) and b < 2):
                    dve.wait_ge(sums_turned[p], b - 1)
                nc.vector.tensor_reduce(sums[:, s, :].rearrange("p (h c) -> p h c", h=H),
                                        prod.rearrange("p h k c -> p h c k"), AX.X, ALU.add)\
                    .then_inc(sums_ready[p], 1)

            def last_front(b, s, K, arrived):
                p, n = 2, 6 * b
                z = weighted[:, 0:K * D].rearrange("p (k c) -> p k c", k=K)
                idl = idle_c[:, 0:K]
                nc.vector.tensor_copy(target_c, one(own[:, bass.ds(b, 1), D:2 * D])).then_inc(front_step[p], 1)
                nc.vector.tensor_scalar(idl, slot_no[:, 0:K], deg[:, bass.ds(b, 1)], NEG, ALU.is_ge, ALU.mult)\
                    .then_inc(front_step[p], 1)
                dve.wait_ge(front_step[p], n + 2)
                dve.wait_ge(rows_in[p][s], arrived)
                nc.vector.tensor_tensor(z, rows_last[:, s, 0:K, D:2 * D],
                                        target_c.unsqueeze(1).to_broadcast([P, K, D]), ALU.add)\
                    .then_inc(front_step[p], 1)
                dve.wait_ge(front_step[p], n + 3)
                nc.vector.scalar_tensor_tensor(out=z, in0=z, scalar=0.0, in1=idl.unsqueeze(2).to_broadcast([P, K, D]),
                                               op0=ALU.max, op1=ALU.add).then_inc(front_step[p], 1)
                dve.wait_ge(front_step[p], n + 4)
                nc.vector.tensor_reduce(top_c, z.rearrange("p k c -> p c k"), AX.X, ALU.max)\
                    .then_inc(front_step[p], 1)
                dve.wait_ge(front_step[p], n + 5)
                nc.vector.tensor_scalar(top_c, top_c, 0.0, None, ALU.max).then_inc(front_step[p], 1)
                dve.wait_ge(front_step[p], n + 6)
                nc.vector.tensor_tensor(z, z, top_c.unsqueeze(1).to_broadcast([P, K, D]), ALU.subtract)\
                    .then_inc(logits_ready[p], 1)

            def last_sums(b, s, K):
                p, n = 2, 7 * b
                z = weighted[:, 0:K * D].rearrange("p (k c) -> p k c", k=K)
                prod = weighted[:, KMAX * D:KMAX * D + K * D].rearrange("p (k c) -> p k c", k=K)
                in_psum, more = min(K, KP), K > KP
                dve.wait_ge(probs_ready[p], 2 * b + 2)
                nc.vector.tensor_tensor(prod[:, 0:in_psum, :], prob_c[:, 0:in_psum, :],
                                        rows_last[:, s, 0:in_psum, 0:D], ALU.mult)\
                    .then_inc(sum_step[p], 1 if more else 2)
                if more:
                    nc.vector.tensor_tensor(prod[:, KP:K, :], z[:, KP:K, :], rows_last[:, s, KP:K, 0:D], ALU.mult)\
                        .then_inc(sum_step[p], 1)
                dve.wait_ge(sum_step[p], n + 2)
                dve.sem_inc(rows_used[p][s], 1)
                nc.vector.tensor_reduce(den_c[:, :], prob_c[:, 0:in_psum, :].rearrange("p k c -> p c k"), AX.X, ALU.add)\
                    .then_inc(sum_step[p], 1 if more else 2)
                if more:
                    nc.vector.tensor_reduce(den_more[:, :], z[:, KP:K, :].rearrange("p k c -> p c k"), AX.X, ALU.add)\
                        .then_inc(sum_step[p], 1)
                nc.vector.tensor_reduce(num_c[:, :], prod.rearrange("p k c -> p c k"), AX.X, ALU.add)\
                    .then_inc(sum_step[p], 1)
                dve.wait_ge(sum_step[p], n + 5)
                if more:
                    nc.vector.scalar_tensor_tensor(out=den_c[:, :], in0=den_c[:, :], scalar=DEN_MIN, in1=den_more[:, :],
                                                   op0=ALU.max, op1=ALU.add).then_inc(sum_step[p], 1)
                else:
                    nc.vector.tensor_scalar(den_c[:, :], den_c[:, :], DEN_MIN, None, ALU.max).then_inc(sum_step[p], 1)
                dve.wait_ge(sum_step[p], n + 6)
                nc.vector.reciprocal(den_c[:, :], den_c[:, :]).then_inc(sum_step[p], 1)
                dve.wait_ge(sum_step[p], n + 7)
                if not (isinstance(b, int) and b < 2):
                    dve.wait_ge(sums_turned[p], b - 1)
                nc.vector.tensor_tensor(sums[:, s, 0:D], num_c[:, :], den_c[:, :], ALU.mult)\
                    .then_inc(sums_ready[p], 1)
                nc.vector.tensor_scalar(sums[:, s, D:2 * D], own[:, bass.ds(b, 1), 0:D].rearrange("p a c -> p (a c)"),
                                        has_edge[:, bass.ds(b, 1)], None, ALU.mult).then_inc(sums_ready[p], 1)

            def norm_stats(p, n, b, s):
                dve.wait_ge(mixed[p], n + 1)
                if not (isinstance(n, int) and n < 2):
                    dve.wait_ge(normed[p], n - 1)
                nc.vector.tensor_tensor(pre[:, s, :], bank_o[s][:, 0:D], one(own[:, bass.ds(b, 1), 0:D]), ALU.add)\
                    .then_inc(mixed_read[p], 1)
                dve.wait_ge(mixed_read[p], n + 1)
                nc.vector.bn_stats(stat[:, :], pre[:, s, :]).then_inc(stat_step[p], 1)
                dve.wait_ge(stat_step[p], n + 1)
                dve.sem_inc(dve_go, 1)
                nc.vector.bn_aggr(mean_var[:, s, :], stat[:, :]).then_inc(stats_ready[p], 1)

            def norm_row(p, n, s, written):
                dve.wait_ge(std_ready[p], n + 1)
                nc.vector.reciprocal(inv_std[:, :], std[:, s:s + 1]).then_inc(norm_step[p], 1)
                dve.wait_ge(norm_step[p], n + 1)
                if not (isinstance(written, int) and written == 0):
                    dve.wait_ge(row_out[p][s], 16 * written)
                nc.vector.tensor_scalar(row[:, s, 0:D], pre[:, s, :], mean_var[:, s, 0:1], inv_std[:, 0:1],
                                        ALU.subtract, ALU.mult).then_inc(normed[p], 1)

            turn = dve.alloc_register("dve_turn")
            dve.reg_mov(turn, 0)

            def heavy_round(p, b, g):
                C, n = (H, 10 * g) if p < 2 else (D, 10 * g)
                lg = logit[:, :, :] if p < 2 else weighted[:, 0:(KMAX + 1) * D].rearrange("p (k c) -> p k c", c=D)
                pr = heavy_prob[:, :, :] if p < 2 else lg
                lk = lg[:, 0:KMAX, :]
                rows = rows_of[p][:, 0, :, :]
                if p < 2:
                    theirs, mine = rows[:, :, D:D + H], own[:, bass.ds(b, 1), OWN[p] + D + H:OWN[p] + TW]
                else:
                    theirs, mine = rows[:, :, D:2 * D], own[:, bass.ds(b, 1), D:2 * D]
                nc.vector.tensor_copy(heavy_at_i[:, :], heavy_at[:, :]).then_inc(heavy_staged, 1)
                dve.wait_ge(heavy_arrived, g + 1)
                nc.vector.tensor_tensor(lk, theirs, mine.to_broadcast([P, KMAX, C]), ALU.add).then_inc(heavy_step, 1)
                nc.vector.tensor_scalar(idle[:, :], slot_no[:, :], heavy_left[:, 0:1], NEG, ALU.is_ge, ALU.mult)\
                    .then_inc(heavy_step, 1)
                dve.wait_ge(heavy_step, n + 2)
                idl = idle[:, :].unsqueeze(2).to_broadcast([P, KMAX, C])
                if p < 2:
                    nc.vector.scalar_tensor_tensor(out=lk, in0=lk, scalar=SLOPE, in1=lk, op0=ALU.mult, op1=ALU.max)\
                        .then_inc(heavy_step, 1)
                    dve.wait_ge(heavy_step, n + 3)
                    nc.vector.tensor_tensor(lk, lk, idl, ALU.add).then_inc(heavy_step, 1)
                else:
                    nc.vector.scalar_tensor_tensor(out=lk, in0=lk, scalar=0.0, in1=idl, op0=ALU.max, op1=ALU.add)\
                        .then_inc(heavy_step, 2)
                dve.wait_ge(heavy_step, n + 4)
                nc.vector.tensor_reduce(heavy_part[:, 0:C], lk.rearrange("p k c -> p c k"), AX.X, ALU.max)\
                    .then_inc(heavy_step, 1)
                dve.wait_ge(heavy_step, n + 5)
                nc.vector.tensor_tensor(heavy_part[:, 0:C], heavy_part[:, 0:C], heavy_top[:, 0:C], ALU.max)\
                    .then_inc(heavy_step, 1)
                dve.wait_ge(heavy_step, n + 6)
                nc.vector.tensor_tensor(lg[:, KMAX, :], heavy_top[:, 0:C], heavy_part[:, 0:C], ALU.subtract)\
                    .then_inc(heavy_step, 1)
                dve.wait_ge(heavy_step, n + 7)
                nc.vector.tensor_copy(heavy_top[:, 0:C], heavy_part[:, 0:C]).then_inc(heavy_step, 1)
                dve.wait_ge(heavy_step, n + 8)
                nc.vector.tensor_tensor(lk, lk, heavy_top[:, 0:C].unsqueeze(1).to_broadcast([P, KMAX, C]),
                                        ALU.subtract).then_inc(heavy_logits, 1)
                dve.wait_ge(heavy_probs, g + 1)
                k = pr[:, 0:KMAX, :]
                rose = pr[:, KMAX, :]
                m = 8 * g
                nc.vector.tensor_tensor(heavy_den[:, 0:C], heavy_den[:, 0:C], rose, ALU.mult).then_inc(heavy_sum, 1)
                nc.vector.tensor_reduce(heavy_part[:, 0:C], k.rearrange("p k c -> p c k"), AX.X, ALU.add)\
                    .then_inc(heavy_sum, 1)
                if p < 2:
                    acc = sums[:, 0, :].rearrange("p (h c) -> p h c", h=H)
                    rise = rose.unsqueeze(2).to_broadcast([P, H, D])
                    prod = weighted[:, 0:H * KMAX * D].rearrange("p (h k c) -> p h k c", h=H, k=KMAX)
                    nc.vector.tensor_tensor(prod, rows[:, :, 0:D].unsqueeze(1).to_broadcast([P, H, KMAX, D]),
                                            k.rearrange("p k h -> p h k").unsqueeze(3).to_broadcast([P, H, KMAX, D]),
                                            ALU.mult).then_inc(heavy_sum, 1)
                    more, parts = sums[:, 1, :].rearrange("p (h c) -> p h c", h=H), prod.rearrange("p h k c -> p h c k")
                else:
                    acc, rise = sums[:, 0, 0:D], rose
                    prod = weighted[:, (KMAX + 1) * D:(2 * KMAX + 1) * D].rearrange("p (k c) -> p k c", c=D)
                    nc.vector.tensor_tensor(prod, rows[:, :, 0:D], k, ALU.mult).then_inc(heavy_sum, 1)
                    more, parts = sums[:, 1, 0:D], prod.rearrange("p k c -> p c k")
                nc.vector.tensor_tensor(acc, acc, rise, ALU.mult).then_inc(heavy_sum, 1)
                dve.wait_ge(heavy_sum, m + 4)
                nc.vector.tensor_tensor(heavy_den[:, 0:C], heavy_den[:, 0:C], heavy_part[:, 0:C], ALU.add)\
                    .then_inc(heavy_sum, 1)
                nc.vector.tensor_reduce(more, parts, AX.X, ALU.add).then_inc(heavy_sum, 1)
                dve.wait_ge(heavy_sum, m + 6)
                nc.vector.tensor_tensor(acc, acc, more, ALU.add).then_inc(heavy_sum, 1)
                nc.vector.tensor_scalar(heavy_at[:, :], heavy_at[:, :], float(KMAX), float(E), ALU.add, ALU.min)\
                    .then_inc(heavy_step, 1)
                nc.vector.tensor_scalar(heavy_left[:, :], heavy_left[:, :], -float(KMAX), None, ALU.add)\
                    .then_inc(heavy_step, 1)
                dve.wait_ge(heavy_step, n + 10)
                dve.sem_inc(heavy_sum, 1)
                dve.wait_ge(heavy_sum, m + 8)

            def heavy_blocks(p):
                for s in range(2):
                    dve.wait_ge(row_out[p][s], 16 * (NB // 2))
                if p < 2:
                    dve.wait_ge(own_ready[p], (1 + p) * NB)
                with dve.If(dve.value_load(most_rounds[0:1, 0:1], min_val=0, max_val=E) > 0):
                    done = dve.alloc_register(f"dve_done{p}")
                    dve.reg_mov(done, 0)
                    with dve.Fori(0, NB) as b:
                        n_rounds = dve.value_load(rounds[0:1, bass.ds(b, 1)], min_val=0, max_val=E)
                        with dve.If(n_rounds > 0):
                            h = dve.snap(done, min_val=0, max_val=NB)
                            n = h + NB
                            nc.vector.tensor_copy(heavy_at[:, :], start_of[:, bass.ds(b, 1)]).then_inc(heavy_init[p], 1)
                            nc.vector.tensor_copy(heavy_left[:, :], deg[:, bass.ds(b, 1)]).then_inc(heavy_init[p], 1)
                            nc.vector.memset(heavy_top[:, :], LOW if p < 2 else 0.0).then_inc(heavy_init[p], 1)
                            nc.vector.memset(heavy_den[:, :], 0.0).then_inc(heavy_init[p], 1)
                            nc.vector.memset(sums[:, 0, :], 0.0).then_inc(heavy_init[p], 1)
                            dve.wait_ge(heavy_init[p], 5 * h + 5)
                            if p == 1:
                                dve.wait_ge(heavy_own, 32 * h + 32)
                            dve.sem_inc(dve_go, 1)
                            with dve.Fori(0, n_rounds) as r:
                                heavy_round(p, b, dve.snap(turn, min_val=0, max_val=3 * E))
                                dve.reg_add(turn, turn, 1)
                            e = 2 * h
                            if p < 2:
                                nc.vector.tensor_scalar(heavy_den[:, 0:H], heavy_den[:, 0:H], ALPHA_EPS, float(H),
                                                        ALU.add, ALU.mult).then_inc(heavy_end[p], 1)
                                dve.wait_ge(heavy_end[p], e + 1)
                                nc.vector.reciprocal(scale[:, :], heavy_den[:, 0:H]).then_inc(heavy_end[p], 1)
                                dve.wait_ge(heavy_end[p], e + 2)
                                acc = sums[:, 0, :].rearrange("p (h c) -> p h c", h=H)
                                nc.vector.tensor_tensor(acc, acc, scale[:, :].unsqueeze(2).to_broadcast([P, H, D]),
                                                        ALU.mult).then_inc(sums_ready[p], 1)
                            else:
                                nc.vector.tensor_scalar(heavy_den[:, :], heavy_den[:, :], 0.5, None, ALU.max)\
                                    .then_inc(heavy_end[p], 1)
                                dve.wait_ge(heavy_end[p], e + 1)
                                nc.vector.reciprocal(heavy_den[:, :], heavy_den[:, :]).then_inc(heavy_end[p], 1)
                                dve.wait_ge(heavy_end[p], e + 2)
                                nc.vector.tensor_tensor(sums[:, 0, 0:D], sums[:, 0, 0:D], heavy_den[:, :], ALU.mult)\
                                    .then_inc(sums_ready[p], 1)
                                nc.vector.tensor_scalar(sums[:, 0, D:2 * D], one(own[:, bass.ds(b, 1), 0:D]),
                                                        has_edge[:, bass.ds(b, 1)], None, ALU.mult)\
                                    .then_inc(sums_ready[p], 1)
                            if p > 0:
                                norm_stats(p, n, b, 0)
                                norm_row(p, n, 0, NB // 2)
                            dve.wait_ge(heavy_out[p], 16 * h + 16)
                            dve.reg_add(done, done, 1)

            for p in range(3):
                for run in RUNS:
                    with pairs_of(dve, run) as u:
                        for s in range(2):
                            b, K = 2 * u + s, run[2][s]
                            if p < 2:
                                gat_front(p, b, s, K, landed(run, s, u))
                            else:
                                last_front(b, s, K, landed(run, s, u))
                            if p > 0 and run[0] > 0:
                                norm_row(p, b - 2, s, u - 1)
                            if p < 2:
                                gat_sums(p, b, s, K)
                            else:
                                last_sums(b, s, K)
                            if p > 0 and (run[0] > 0 or s == 1):
                                norm_stats(p, b - 1, b - 1, 1 - s)
                if p > 0:
                    norm_row(p, NB - 2, 0, NB // 2 - 1)
                    norm_stats(p, NB - 1, NB - 1, 1)
                    norm_row(p, NB - 1, 1, NB // 2 - 1)
                heavy_blocks(p)

        @block.scalar
        def _(act):
            def stage_x(j):
                nc.scalar.activation(x7[:, :, :], x_tab[:, bass.ds(7 * j, 7), 0:D], ACT.Copy).then_inc(x_staged, 1)

            def coefficients(j, last=False):
                act.wait_ge(x_turned, j + 1)
                nc.scalar.activation(xT7[:, :], bank_t[0:D, 0:7 * P], ACT.Copy).then_inc(x_turned_copied, 1)
                if not last:
                    stage_x(j + 1)
                act.wait_ge(coef_made, j + 1)
                nc.scalar.activation(x_tab[:, bass.ds(7 * j, 7), D:TW],
                                     bank_a[:, 0:7 * 2 * H].rearrange("p (b c) -> p b c", b=7), ACT.Copy)\
                    .then_inc(coef_stored, 1)

            def stage_entries(j, k):
                act.wait_ge(coef_stored, j + 1)
                nc.scalar.activation(order_now[:, 7 * k:7 * k + 7], order_at[:, bass.ds(7 * j, 7)], ACT.Copy)\
                    .then_inc(entry_staged[k], 1)
                nc.scalar.activation(stage_e[:, 7 * k:7 * k + 7, :], x_tab[:, bass.ds(7 * j, 7), :], ACT.Copy)\
                    .then_inc(entry_staged[k], 1)

            act.wait_ge(prep_step, 5)
            nc.scalar.activation(below[:, COLS_V, 0:1], node_half[:, 0:1], ACT.Sign).then_inc(counted_a, COLS - COLS_V)
            act.wait_ge(counted_a, COLS - COLS_V)
            for first, last in ((0, 0), (1, 2)):
                for k in range(first, last + 1):
                    act.wait_ge(window_in[k], 16 * (PARTS[k][1] - PARTS[k][0]))
                with act.Fori(PARTS[first][0], PARTS[last][1]) as g:
                    for c in range(COLS_V, COLS):
                        done = (COLS - COLS_V) * g + c - COLS_V
                        act.wait_ge(counted_a, done + 1)
                        nc.scalar.activation(below[:, c, :], one(windows[:, bass.ds(g, 1), :]), ACT.Sign,
                                             bias=node_half[:, bass.ds(COLS * g + c, 1)], scale=-1.0,
                                             accum_out=sign_sum[:, bass.ds(done, 1)]).then_inc(counted_a, 1)
            act.wait_ge(x_in, 32)
            stage_x(0)
            coefficients(0)
            act.wait_ge(places_ready, 5)
            stage_entries(0, 0)
            coefficients(1)
            stage_entries(1, 1)
            def next_entries(j, last=False):
                for k in range(2):
                    coefficients(2 * j + k, last and k == 1)
                    act.wait_ge(entry_out[k], 112 * j)
                    stage_entries(2 * j + k, k)

            with act.Fori(1, NB // 14 - 1) as j:
                next_entries(j)
            next_entries(NB // 14 - 1, last=True)

            def stage_sources(p, b, s):
                nc.scalar.activation(idx_now[:, s, :], idx_all[:, bass.ds(b, 1), :].rearrange("p a k -> p (a k)"),
                                     ACT.Copy).then_inc(idx_ready[p][s], 1)

            def stage_start(b, s):
                nc.scalar.activation(start_now[:, s:s + 1], own[:, bass.ds(b, 1), START], ACT.Copy)\
                    .then_inc(start_staged[s], 1)

            def keep_places(b, s, K):
                nc.scalar.activation(one(idx_all[:, bass.ds(b, 1), 0:K]), rows_1[:, s, 0:K, PLACE], ACT.Copy)\
                    .then_inc(places_kept[s], 1)

            def exponentials(p, b, K):
                act.wait_ge(logits_ready[p], b + 1)
                if p < 2:
                    nc.scalar.activation(prob[:, 0:K, :], logit[:, 0:K, :], ACT.Exp).then_inc(probs_ready[p], 1)
                else:
                    z = weighted[:, 0:K * D].rearrange("p (k c) -> p k c", c=D)
                    nc.scalar.activation(prob_c[:, 0:min(K, KP), :], z[:, 0:min(K, KP), :], ACT.Exp)\
                        .then_inc(probs_ready[p], 1 if K > KP else 2)
                    if K > KP:
                        nc.scalar.activation(z[:, KP:K, :], z[:, KP:K, :], ACT.Exp).then_inc(probs_ready[p], 1)

            def stage_own(p, n, b, s):
                if not (isinstance(n, int) and n < 2):
                    act.wait_ge(sums_turned[p], n - 1)
                nc.scalar.activation(own_now[:, s, :], one(own[:, bass.ds(b, 1), OWN[p]:OWN[p] + D]), ACT.Copy)\
                    .then_inc(own_staged[p], 1)

            def copy_turned(p, n):
                act.wait_ge(sums_turned[p], n + 1)
                if not (isinstance(n, int) and n == 0):
                    act.wait_ge(mixed[p], n)
                if p < 2:
                    nc.scalar.activation(turned[:, :], bank_v[:, 0:2 * P], ACT.Copy).then_inc(turned_copied[p], 1)
                    nc.scalar.activation(own_turned[0:D, :], bank_v[0:D, 2 * P:3 * P], ACT.Copy)\
                        .then_inc(turned_copied[p], 1)
                else:
                    nc.scalar.activation(turned[:, 0:P], bank_v[:, 0:P], ACT.Copy).then_inc(turned_copied[p], 2)

            def copy_row_turned(p, n):
                act.wait_ge(row_in_pe[p], n + 1)
                if not (isinstance(n, int) and n == 0):
                    act.wait_ge(extra_made[p], n)
                nc.scalar.activation(row_turned[0:D, :], bank_h[0:D, 0:P], ACT.Copy).then_inc(row_copied[p], 1)

            def gat1_row(n, b, s, written):
                act.wait_ge(mixed[0], n + 1)
                if not (isinstance(written, int) and written == 0):
                    act.wait_ge(row_out[0][s], 16 * written)
                nc.scalar.activation(row[:, s, 0:D], bank_o[s][:, 0:D], ACT.Relu).then_inc(mixed_read[0], 1)
                copy_row_turned(0, n)
                act.wait_ge(extra_made[0], n + 1)
                nc.scalar.activation(row[:, s, D:TW], bank_a[:, 0:2 * H], ACT.Copy).then_inc(row_ready[0], 1)
                act.wait_ge(row_ready[0], n + 1)
                nc.scalar.activation(one(own[:, bass.ds(b, 1), TX:OW]), row[:, s, 0:TW], ACT.Copy)\
                    .then_inc(own_ready[0], 1)

            def gat2_row(n, b, s):
                copy_row_turned(1, n)
                act.wait_ge(extra_made[1], n + 1)
                nc.scalar.activation(row[:, s, D:2 * D], bank_a[:, 0:D], ACT.Copy).then_inc(row_ready[1], 1)
                nc.scalar.activation(one(own[:, bass.ds(b, 1), D:2 * D]), bank_a[:, D:2 * D], ACT.Copy)\
                    .then_inc(own_ready[1], 1)
                nc.scalar.activation(one(own[:, bass.ds(b, 1), 0:D]), row[:, s, 0:D], ACT.Copy)\
                    .then_inc(own_ready[1], 1)

            def last_row(n, b, s):
                act.wait_ge(normed[2], n + 1)
                nc.scalar.activation(node_now[:, s:s + 1], node_of[:, bass.ds(b, 1)], ACT.Copy)\
                    .then_inc(row_ready[2], 1)

            def deviation(p, n, s):
                act.wait_ge(stats_ready[p], n + 1)
                nc.scalar.activation(std[:, s:s + 1], mean_var[:, s, 1:2], ACT.Sqrt, bias=eps[:, 0:1])\
                    .then_inc(std_ready[p], 1)

            def finish_row(p, n, b, s):
                if p == 1:
                    gat2_row(n, b, s)
                else:
                    last_row(n, b, s)

            def heavy_blocks(p):
                for s in range(2):
                    act.wait_ge(row_out[p][s], 16 * (NB // 2))
                with act.If(act.value_load(most_rounds[0:1, 0:1], min_val=0, max_val=E) > 0):
                    done = act.alloc_register(f"act_done{p}")
                    act.reg_mov(done, 0)
                    with act.Fori(0, NB) as b:
                        n_rounds = act.value_load(rounds[0:1, bass.ds(b, 1)], min_val=0, max_val=E)
                        with act.If(n_rounds > 0):
                            h = act.snap(done, min_val=0, max_val=NB)
                            n = h + NB
                            if p == 1:
                                act.wait_ge(heavy_own, 32 * h + 32)
                            if p < 2:
                                stage_own(p, n, b, 0)
                            with act.Fori(0, n_rounds) as r:
                                g = act.snap(turn, min_val=0, max_val=3 * E)
                                act.wait_ge(heavy_logits, g + 1)
                                if p < 2:
                                    nc.scalar.activation(heavy_prob[:, :, :], logit[:, :, :], ACT.Exp)\
                                        .then_inc(heavy_probs, 1)
                                else:
                                    nc.scalar.activation(weighted[:, 0:(KMAX + 1) * D], weighted[:, 0:(KMAX + 1) * D],
                                                         ACT.Exp).then_inc(heavy_probs, 1)
                                act.reg_add(turn, turn, 1)
                            copy_turned(p, n)
                            if p == 0:
                                gat1_row(n, b, 0, NB // 2)
                            else:
                                deviation(p, n, 0)
                                finish_row(p, n, b, 0)
                            act.wait_ge(heavy_out[p], 16 * h + 16)
                            act.reg_add(done, done, 1)

            turn = act.alloc_register("act_turn")
            act.reg_mov(turn, 0)
            act.wait_ge(own_in[0], 16)
            for b in range(2):
                stage_start(b, b)
            act.wait_ge(own_in[1], 16 * (NB // 14 - 1))
            act.wait_ge(own_padded, 1)
            act.wait_ge(cleared, 6)
            act.wait_ge(degs_ready, 4)
            act.wait_ge(rounds_ready, 1)
            for p in range(3):
                if p > 0:
                    stage_sources(p, 0, 0)
                for run in RUNS:
                    with pairs_of(act, run) as u:
                        for s in range(2):
                            b, K = 2 * u + s, run[2][s]
                            if p == 0:
                                act.wait_ge(idx_in[s], 16 * u + 16)
                                stage_start(b + 2, s)
                            else:
                                if run[0] > 0 or s == 1:
                                    act.wait_ge(rows_in[p][1 - s], landed_before(run, s, u))
                                stage_sources(p, b + 1, 1 - s)
                            exponentials(p, b, K)
                            if p == 0:
                                keep_places(b, s, K)
                            if p < 2:
                                stage_own(p, b, b, s)
                            if run[0] > 0 or s == 1:
                                copy_turned(p, b - 1)
                                if p == 0:
                                    gat1_row(b - 1, b - 1, 1 - s, u - 1 + s)
                            if p > 0 and run[0] > 0:
                                finish_row(p, b - 2, b - 2, s)
                            if p > 0 and (run[0] > 0 or s == 1):
                                deviation(p, b - 1, 1 - s)
                copy_turned(p, NB - 1)
                if p == 0:
                    gat1_row(NB - 1, NB - 1, 1, NB // 2 - 1)
                    act.wait_ge(idx_in[0], 16 * (NB // 2) + 16)
                else:
                    finish_row(p, NB - 2, NB - 2, 0)
                    deviation(p, NB - 1, 1)
                    finish_row(p, NB - 1, NB - 1, 1)
                heavy_blocks(p)

        @block.tensor
        def _(pe):
            pe.wait_ge(consts_ready, 10)
            pe.wait_ge(last_cast, 1)
            nc.tensor.matmul(bank_t[:, 0:512], ones[0:1, :], last_f[:, 0:512], start=True, stop=True)
            nc.tensor.matmul(bank_t[:, 512:NSEG], ones[0:1, :], last_f[:, 512:NSEG], start=True, stop=True)\
                .then_inc(last_spread, 1)
            pe.wait_ge(weights_in, 16 * N_WEIGHT_LOADS)
            nc.tensor.transpose(bank_h[0:D, 0:D], w_lin_in[:, 0:D], ident[0:D, 0:D])
            nc.tensor.transpose(bank_h[0:D, D:2 * D], w_lin_in[:, D:2 * D], ident[0:D, 0:D])
            nc.tensor.transpose(bank_h[:, 2 * D:3 * D], w_out_in[:, :], ident[0:D, 0:D]).then_inc(lin_turned, 1)
            pe.wait_ge(weights_ready, 12)

            def turn_x(j):
                pe.wait_ge(x_staged, j + 1)
                pe.sem_inc(pe_go, 1)
                for c in range(7):
                    last = nc.tensor.transpose(bank_t[0:D, P * c:P * c + P],
                                               x7[:, c, :], ident[:, :])
                last.then_inc(x_turned, 1)

            def make_coef(j):
                pe.wait_ge(x_turned_copied, j + 1)
                for c in range(7):
                    last = nc.tensor.matmul(bank_a[:, 2 * H * c:2 * H * c + 2 * H], xT7[:, P * c:P * c + P],
                                            w_coef[0][:, :], start=True, stop=True)
                last.then_inc(coef_made, 1)

            pe.wait_ge(past_end_found, 1)
            nc.tensor.matmul(bank_s[0:1, 0:1], past_end[:, :], ones[:, 0:1], start=True, stop=True)\
                .then_inc(past_end_summed, 1)
            pe.wait_ge(counts_ready, 2)
            nc.tensor.matmul(bank_s[:, 0:CLS], after[:, :], upto[:, 0:CLS], start=True, stop=False)
            nc.tensor.matmul(bank_s[:, 0:CLS], before[:, :], upto[:, 1:CLS + 1], start=False, stop=True)\
                .then_inc(counts_summed, 1)
            turn_x(0)
            make_coef(0)
            with pe.Fori(1, NB // 7) as j:
                pe.wait_ge(x_turned_copied, j)
                turn_x(j)
                pe.wait_ge(coef_stored, j)
                make_coef(j)

            pe.wait_ge(degs_ready, 4)
            nc.tensor.transpose(bank_s[0:NB, 0:P], deg[:, :], ident[:, :]).then_inc(degs_turned, 1)
            pe.wait_ge(most_found, 1)
            nc.tensor.transpose(bank_s[0:1, 0:NB], most_col[:, :], ident[0:NB, 0:NB]).then_inc(most_turned, 1)

            def turn_sums(p, b, s):
                if p < 2:
                    pe.wait_ge(sums_ready[p], b + 1)
                else:
                    pe.wait_ge(sums_ready[p], 2 * b + 2)
                if not (isinstance(b, int) and b == 0):
                    pe.wait_ge(turned_copied[p], 2 * b)
                pe.sem_inc(pe_go, 1)
                if p < 2:
                    nc.tensor.transpose(bank_v[:, 0:P], sums[:, s, 0:P], ident[:, :])
                    nc.tensor.transpose(bank_v[:, P:2 * P], sums[:, s, P:2 * P], ident[:, :])
                    pe.wait_ge(own_staged[p], b + 1)
                    pe.sem_inc(pe_go, 1)
                    nc.tensor.transpose(bank_v[0:D, 2 * P:3 * P], own_now[:, s, :], ident[:, :])\
                        .then_inc(sums_turned[p], 1)
                else:
                    nc.tensor.transpose(bank_v[:, 0:P], sums[:, s, 0:P], ident[:, :]).then_inc(sums_turned[p], 1)

            def mix(p, b, s):
                pe.wait_ge(turned_copied[p], 2 * b + 2)
                if not (isinstance(b, int) and b < 2):
                    pe.wait_ge(mixed_read[p], b - 1)
                o = bank_o[s][:, 0:D]
                if p < 2:
                    nc.tensor.matmul(o, turned[:, 0:P], w_heads[p][:, 0, :], start=True, stop=False)
                    nc.tensor.matmul(o, turned[:, P:2 * P], w_heads[p][:, 1, :], start=False, stop=False)
                    nc.tensor.matmul(o, own_turned[:, :], w_self[p][:, :], start=False, stop=True)\
                        .then_inc(mixed[p], 1)
                else:
                    nc.tensor.matmul(o, turned[:, 0:P], w_out[:, :], start=True, stop=False)
                    nc.tensor.matmul(o, ones[0:1, :], b_out_row[:, :], start=False, stop=True).then_inc(mixed[p], 1)

            def extend_row(p, b, s):
                if p == 0:
                    pe.wait_ge(mixed_read[0], b + 1)
                else:
                    pe.wait_ge(normed[p], b + 1)
                if not (isinstance(b, int) and b == 0):
                    pe.wait_ge(row_copied[p], b)
                pe.sem_inc(pe_go, 1)
                nc.tensor.transpose(bank_h[0:D, 0:P], row[:, s, 0:D], ident[:, :]).then_inc(row_in_pe[p], 1)
                pe.wait_ge(row_copied[p], b + 1)
                if not (isinstance(b, int) and b == 0):
                    if p == 0:
                        pe.wait_ge(row_ready[0], b)
                    else:
                        pe.wait_ge(own_ready[1], 2 * b)
                if p == 0:
                    nc.tensor.matmul(bank_a[:, 0:2 * H], row_turned[0:D, :], w_coef[1][:, :], start=True, stop=True)\
                        .then_inc(extra_made[p], 1)
                else:
                    nc.tensor.matmul(bank_a[:, 0:2 * D], row_turned[:, :], w_edge[:, :], start=True, stop=True)\
                        .then_inc(extra_made[p], 1)

            def heavy_blocks(p):
                for s in range(2):
                    pe.wait_ge(row_out[p][s], 16 * (NB // 2))
                pe.wait_ge(rounds_ready, 1)
                with pe.If(pe.value_load(most_rounds[0:1, 0:1], min_val=0, max_val=E) > 0):
                    done = pe.alloc_register(f"pe_done{p}")
                    pe.reg_mov(done, 0)
                    with pe.Fori(0, NB) as b:
                        with pe.If(pe.value_load(rounds[0:1, bass.ds(b, 1)], min_val=0, max_val=E) > 0):
                            h = pe.snap(done, min_val=0, max_val=NB)
                            turn_sums(p, h + NB, 0)
                            mix(p, h + NB, 0)
                            if p < 2:
                                extend_row(p, h + NB, 0)
                            pe.wait_ge(heavy_out[p], 16 * h + 16)
                            pe.reg_add(done, done, 1)

            for p in range(3):
                for run in RUNS:
                    with pairs_of(pe, run) as u:
                        for s in range(2):
                            b = 2 * u + s
                            if run[0] > 0 or s == 1:
                                mix(p, b - 1, 1 - s)
                                if p == 0:
                                    extend_row(p, b - 1, 1 - s)
                            if p == 1 and run[0] > 0:
                                extend_row(p, b - 2, s)
                            turn_sums(p, b, s)
                mix(p, NB - 1, 1)
                if p == 0:
                    extend_row(p, NB - 1, 1)
                if p == 1:
                    extend_row(p, NB - 2, 0)
                    extend_row(p, NB - 1, 1)
                heavy_blocks(p)


_INS = ['x', 'src', 'dst', 'L0_gnn_W1', 'L0_gnn_att_src1', 'L0_gnn_att_dst1', 'L0_gnn_b1', 'L0_gnn_lW1', 'L0_gnn_lb1',
        'L0_gnn_W2', 'L0_gnn_att_src2', 'L0_gnn_att_dst2', 'L0_gnn_b2', 'L0_gnn_lW2', 'L0_gnn_lb2',
        'L1_gnn_W_lin', 'L1_gnn_b_lin', 'L1_gnn_W_out', 'L1_gnn_b_out']


def kernel(**inputs):
    import numpy as np
    import concourse.bacc as bacc
    from concourse.bass_utils import run_bass_kernel_spmd

    nc = bacc.Bacc("TRN2", target_bir_lowering=False, num_devices=1)
    arrays, args = {}, []
    for name in _INS:
        a = np.ascontiguousarray(inputs[name])
        arrays[f"in_{name}"] = a
        args.append(nc.dram_tensor(f"in_{name}", a.shape, mybir.dt.from_np(a.dtype), kind="ExternalInput").ap())
    shape = inputs['x'].shape
    args.append(nc.dram_tensor("out_0", shape, F32, kind="ExternalOutput").ap())
    build(nc, *args)
    r = run_bass_kernel_spmd(nc, [arrays], core_ids=[0])
    return r.results[0]["out_0"]
```
